# Optimizing a Trainium2 kernel written in Bass

```python
import numpy as np
import jax
import jax.numpy as jnp

def _softmax(x, axis=-1):
    return jax.nn.softmax(x, axis=axis)
def _gelu(x):
    return jax.nn.gelu(x, approximate=True)
def _silu(x):
    return jax.nn.silu(x)
def _sigmoid(x):
    return jax.nn.sigmoid(x)
def _layernorm(x, axis=-1, eps=1e-5):
    m = jnp.mean(x, axis=axis, keepdims=True)
    v = jnp.var(x, axis=axis, keepdims=True)
    return (x - m) / jnp.sqrt(v + eps)
def _scatter_add(tgt, idx, src, axis=0):
    return tgt.at[idx].add(src)
def _segment_sum(src, seg, n):
    return jax.ops.segment_sum(src, seg, n)

kernel_name = 'mk_conv_preact_d1_conv_nchw512_d28a3c'

def setup_inputs(seed: int = 0):
    np.random.seed(seed)
    _w = jnp.asarray
    def _rec_inputs():
        import jax
        import jax.numpy as jnp
        _gk = jax.random.key(seed)
        x = -0.0002928 + 1 * jax.random.normal(jax.random.fold_in(_gk, 1), (4, 512, 64, 32), jnp.float32)
        return x
    x = _rec_inputs()
    def _L0_conv_setup():
        import jax, jax.numpy as jnp
        import numpy as np
        HEADS = 8
        EPS = 1e-05

        def _layernorm(x, gamma, beta):
            mu = jnp.mean(x, axis=-1, keepdims=True)
            var = jnp.var(x, axis=-1, keepdims=True)
            return (x - mu) * jax.lax.rsqrt(var + EPS) * gamma + beta
        key = jax.random.key(seed)
        ks = jax.random.split(key, 4)
        dim = 512
        x = jax.random.normal(ks[0], (4, dim, 64, 32), dtype=jnp.float32)
        w_qkv = jax.random.normal(ks[1], (dim, 3 * dim), dtype=jnp.float32) * dim ** (-0.5)
        b_qkv = jnp.zeros((3 * dim,), jnp.float32)
        w_out = jax.random.normal(ks[2], (dim, dim), dtype=jnp.float32) * dim ** (-0.5)
        b_out = jnp.zeros((dim,), jnp.float32)
        gamma1 = jnp.ones((dim,), jnp.float32)
        beta1 = jnp.zeros((dim,), jnp.float32)
        gamma2 = jnp.ones((dim,), jnp.float32)
        beta2 = jnp.zeros((dim,), jnp.float32)
        return {'x': x, 'w_qkv': w_qkv, 'b_qkv': b_qkv, 'w_out': w_out, 'b_out': b_out, 'gamma1': gamma1, 'beta1': beta1, 'gamma2': gamma2, 'beta2': beta2}
    _L0_conv_all = _L0_conv_setup()
    _L0_conv_in = {k: v for k, v in _L0_conv_all.items() if k in ('w_qkv', 'b_qkv', 'w_out', 'b_out', 'gamma1', 'beta1', 'gamma2', 'beta2', )}
    del _L0_conv_all

    return {
        "x": x,
        "L0_conv_w_qkv": _L0_conv_in["w_qkv"],
        "L0_conv_b_qkv": _L0_conv_in["b_qkv"],
        "L0_conv_w_out": _L0_conv_in["w_out"],
        "L0_conv_b_out": _L0_conv_in["b_out"],
        "L0_conv_gamma1": _L0_conv_in["gamma1"],
        "L0_conv_beta1": _L0_conv_in["beta1"],
        "L0_conv_gamma2": _L0_conv_in["gamma2"],
        "L0_conv_beta2": _L0_conv_in["beta2"],
    }

def reference(x, L0_conv_w_qkv, L0_conv_b_qkv, L0_conv_w_out, L0_conv_b_out, L0_conv_gamma1, L0_conv_beta1, L0_conv_gamma2, L0_conv_beta2):
    import jax
    import jax.numpy as jnp
    def _L0_conv_ref(x, w_qkv, b_qkv, w_out, b_out, gamma1, beta1, gamma2, beta2):
        import jax, jax.numpy as jnp
        import numpy as np
        HEADS = 8
        EPS = 1e-05

        def _layernorm(x, gamma, beta):
            mu = jnp.mean(x, axis=-1, keepdims=True)
            var = jnp.var(x, axis=-1, keepdims=True)
            return (x - mu) * jax.lax.rsqrt(var + EPS) * gamma + beta
        b, c, f, t = x.shape
        h = HEADS
        dh = c // h
        scale = dh ** (-0.5)
        xp = jnp.transpose(x, (0, 2, 3, 1))
        xn = _layernorm(xp, gamma1, beta1)
        qkv = xn @ w_qkv + b_qkv
        q, k, v = jnp.split(qkv, 3, axis=-1)

        def to_heads(u):
            return jnp.transpose(u.reshape(b, f * t, h, dh), (0, 2, 1, 3))
        q, k, v = (to_heads(q), to_heads(k), to_heads(v))
        scores = jnp.einsum('bhqd,bhkd->bhqk', q, k) * scale
        attn = jax.nn.softmax(scores, axis=-1)
        o = jnp.einsum('bhqk,bhkd->bhqd', attn, v)
        o = jnp.transpose(o, (0, 2, 1, 3)).reshape(b, f, t, c)
        o = _layernorm(o, gamma2, beta2)
        o = o @ w_out + b_out
        o = o + xn
        return jnp.transpose(o, (0, 3, 1, 2))

    def _gn(v, G=32, eps=1e-5):
        B_, C_, H_, W_ = v.shape
        g = v.reshape(B_, G, C_ // G, H_, W_)
        m = jnp.mean(g, axis=(2, 3, 4), keepdims=True)
        s = jnp.var(g, axis=(2, 3, 4), keepdims=True)
        return ((g - m) / jnp.sqrt(s + eps)).reshape(v.shape)

    def _ln_c(v, eps=1e-6):
        m = jnp.mean(v, axis=1, keepdims=True)
        s = jnp.var(v, axis=1, keepdims=True)
        return (v - m) / jnp.sqrt(s + eps)

    def _ln_t(v, eps=1e-5):
        m = jnp.mean(v, axis=-1, keepdims=True)
        s = jnp.var(v, axis=-1, keepdims=True)
        return (v - m) / jnp.sqrt(s + eps)

    def _to_tokens(v):
        B_, C_, H_, W_ = v.shape
        return v.reshape(B_, C_, H_ * W_).transpose(0, 2, 1)
    def _from_tokens(t, like):
        B_, C_, H_, W_ = like.shape
        return t.transpose(0, 2, 1).reshape(B_, C_, H_, W_)

    x = x + _L0_conv_ref(_gn(x), L0_conv_w_qkv, L0_conv_b_qkv, L0_conv_w_out, L0_conv_b_out, L0_conv_gamma1, L0_conv_beta1, L0_conv_gamma2, L0_conv_beta2)
    return x


_drawn_inputs = setup_inputs


def setup_inputs(seed=0):
    import zlib

    import numpy as np

    out = dict(_drawn_inputs(seed))
    spreads = {'L0_conv_b_qkv': (0.0, 0.1),
     'L0_conv_b_out': (0.0, 0.1),
     'L0_conv_gamma1': (1.0, 0.2),
     'L0_conv_beta1': (0.0, 0.1),
     'L0_conv_gamma2': (1.0, 0.2),
     'L0_conv_beta2': (0.0, 0.1)}
    factors = {}
    for name, (base, spread) in spreads.items():
        noise = np.random.default_rng([zlib.crc32(name.encode()), seed]).standard_normal(out[name].shape)
        drawn = base * np.exp(spread * noise) if base else spread * noise
        out[name] = jnp.asarray(drawn.astype(out[name].dtype))
    for name, factor in factors.items():
        out[name] = (out[name] * factor).astype(out[name].dtype)
    return out
```

```python
import concourse.bass as bass
from concourse import mybir
from contextlib import ExitStack

F32 = mybir.dt.float32
F32R = mybir.dt.float32r
ALU = mybir.AluOpType
ACT = mybir.ActivationFunctionType
AX = mybir.AxisListType

P = 128
BATCH, C, T = 4, 512, 2048
HEADS = 8
DH = C // HEADS
SCALE = float(DH) ** -0.5
EPS = 1e-5
GROUP = C // 32
NK = C // P
W = 512
NT = T // W
KB = T // P
UPB = KB // 2
UNITS = NT * UPB
LAG = 2

BANK_S = [0, 1, 2]
BANK_PROJ = 3
BANK_MX = [4, 5]
BANK_PV = 6
BANK_MISC = 7

AHEAD = UPB // 2
QK_PROJ = {4 * t + i: (t, i, 3) for t in range(NT) for i in range(3)}
V_PROJ = {16 + 2 * t + i: (t, i, 2) for t in range(NT) for i in range(2)}
V_TURN = [{16 + 2 * t: t for t in range(NT)},
          {24 + 2 * t: t for t in range(NT)}]
LOAD_WEIGHTS, SPLIT_QK, SPLIT_V = 16, 21, 23
NM_TURN = {UPB * n + AHEAD: n + 1 for n in range(NT)}
FOLD = {UPB * n + LAG: n - 1 for n in range(NT)}
OPEN = 4


def max_steps(slot, u):
    n, s = divmod(2 * (u + AHEAD), 4 * NT)
    return [(*divmod(n + 1, NT), s + i) for i in range(2)] if n + 1 < NT or slot.has_next else []


def ended(plan, u):
    t, part, parts = plan.get(u - 1, (0, 0, 2))
    return t if part == parts - 1 else None


PRO_MX = 24
SLOT_MX = 4 * KB
BATCH_MX = SLOT_MX * HEADS


class Slot:

    def __init__(self, b, p, odd, last_pair=False, first=False):
        self.odd, self.first = odd, first
        self.has_next, self.has_pair = not (last_pair and odd), not last_pair
        self.h = b * HEADS + p * 2 + odd
        self.pair = b * (HEADS // 2) + p
        self.units = self.h * UNITS
        self.mx = b * BATCH_MX + p * (2 * SLOT_MX) + (PRO_MX + odd * SLOT_MX)
        self.mx_half = b * (BATCH_MX // 2) + p * SLOT_MX + (PRO_MX + odd * SLOT_MX) // 2

    def two_before(self, u):
        return self.units + (u - 1 if u > 1 or not self.first else 0)


def opening(b):
    return [(Slot(b, 0, 0, first=True), u) for u in range(OPEN)]


def turn(b, p, last_pair=False):
    even, odd = Slot(b, p, 0, last_pair, first=True), Slot(b, p, 1, last_pair)
    units = [(even, u) for u in range(OPEN, UNITS)] + [(odd, u) for u in range(UNITS)]
    return units + ([] if last_pair else [(Slot(b, p + 1, 0), u) for u in range(OPEN)])


def program(nc, x, w_qkv, b_qkv, w_out, b_out, gamma1, beta1, gamma2, beta2, out):
    x_v = x.rearrange("b (k p) f t -> b p k (f t)", p=P)
    out_v = out.rearrange("b (k p) f t -> b p k (f t)", p=P)
    w_v = w_qkv.rearrange("(k p) n -> p k n", p=P)
    wo_v = w_out.rearrange("(k p) n -> p k n", p=P)
    z_dram = nc.dram_tensor("z_scratch", (BATCH, P, NK, T), F32, kind="Internal").ap()
    o_dram = nc.dram_tensor("o_scratch", (BATCH, T, C), F32, kind="Internal").ap()
    o_v = o_dram.rearrange("b (t p) c -> b p t c", p=P)

    ctx = ExitStack()
    with ctx:
        def sb(name, shape, dt=F32):
            return ctx.enter_context(nc.sbuf_tensor(name, shape, dt))

        def sem(name):
            return ctx.enter_context(nc.semaphore(name))

        with ExitStack() as shared:
            xb = shared.enter_context(nc.sbuf_tensor("xb", [P, NK, T], F32))
            gb = shared.enter_context(nc.sbuf_tensor("gb", [P, NK, T], F32))
        with ExitStack() as shared:
            shared.enter_context(nc.sbuf_tensor("behind_xb", [P, NK * T], F32))
            ob = shared.enter_context(nc.sbuf_tensor("ob", [P, KB, C], F32))
        k_hl, k_h1, q_hh, q_lm = [], [], [], []
        for s in range(2):
            k_hl.append(sb(f"k_hl{s}", [P, T], F32R))
            k_h1.append(sb(f"k_h1{s}", [P, T], F32R))
            q_hh.append(sb(f"q_hh{s}", [P, T], F32R))
            q_lm.append(sb(f"q_lm{s}", [P, T], F32R))
        xh = sb("xh", [P, NK, T], F32R)
        xl = sb("xl", [P, NK, T], F32R)
        v_hl = sb("v_hl", [P, 2, KB, P], F32R)
        vt = sb("vt", [P, T])
        probs = sb("probs", [P, 2, 2 * W])
        ph = sb("ph", [P, 2, 2 * W], F32R)
        pl = sb("pl", [P, 2, 2 * W], F32R)
        acc = sb("acc", [P, 2, W])
        wq_raw = sb("wq_raw", [P, NK, P])
        wq_h = sb("wq_h", [P, NK, P], F32R)
        wq_l = sb("wq_l", [P, NK, P], F32R)
        wv_raw = sb("wv_raw", [P, NK, P])
        wv_h = sb("wv_h", [P, NK, P], F32R)
        wv_l = sb("wv_l", [P, NK, P], F32R)
        b_qk = sb("b_qk", [P, 1])
        b_v = sb("b_v", [P, 1])
        ot = sb("ot", [P, W])
        rs = sb("rs", [P, 2, W])
        o_st = sb("o_st", [P, 2, 4, DH])
        nm4 = sb("nm4", [P, 2, 4, NT])
        nm = sb("nm", [P, 2, 4])
        nm_t = sb("nm_t", [4, 2, P], F32R)
        rden = sb("rden", [P, 4])
        carrier = sb("carrier", [P, 1])
        ident = sb("ident", [P, P])
        fold = sb("fold", [P, DH])
        ones = sb("ones", [P, 1])
        zero = sb("zero", [P, 1])
        avg_c = sb("avg_c", [P, P])
        avg_g = sb("avg_g", [P, P])
        par = sb("par", [P, 5, NK])
        bn = sb("bn", [P, NK, NT, 6])
        mv = sb("mv", [P, NK, 2])
        gm = sb("gm", [P, NK])
        gv = sb("gv", [P, NK])
        gs = sb("gs", [P, NK])
        bn2 = sb("bn2", [P, KB, 6])
        mv2 = sb("mv2", [P, KB, 2])
        rs2 = sb("rs2", [P, KB])
        sq = probs[:, :, :].rearrange("p a (k w) -> p (a k) w", w=W)
        on_st = [acc[:, 0, :], acc[:, 1, :], rs[:, 0, :], rs[:, 1, :]]
        inv = on_st
        wo_raw, wo_h, wo_l = (t[:, :, :].rearrange("p a (k w) -> p (a k) w", w=W) for t in (probs, ph, pl))
        z_st = vt[:, :].rearrange("p (k w) -> p k w", w=W)

        ps = ctx.enter_context(nc.psum_tensor("ps", [P, 8, W], F32))

        const_set, const_ready, fold_ready, par_in = sem("const_set"), sem("const_ready"), sem("fold_ready"), sem("par_in")
        x_in = [sem(f"x_in{k}") for k in range(NK)]
        bn_done, bn_agg = sem("bn_done"), sem("bn_agg")
        gn_in, gn_sum, gn_dve, gn_std = sem("gn_in"), sem("gn_sum"), sem("gn_dve"), sem("gn_std")
        g_ready, mean_ready, dev_ready, sq_ready = sem("g_ready"), sem("mean_ready"), sem("dev_ready"), sem("sq_ready")
        var_ready, veps_ready, std_ready, inv_ready = sem("var_ready"), sem("veps_ready"), sem("std_ready"), sem("inv_ready")
        norm_ready, xn_ready, xh_ready, xl_ready = sem("norm_ready"), sem("xn_ready"), sem("xh_ready"), sem("xl_ready")
        z_ready, z_out, rows_set = sem("z_ready"), sem("z_out"), sem("rows_set")
        wq_in, wq_hi, wq_lo = sem("wq_in"), sem("wq_hi"), sem("wq_lo")
        wv_in, wv_hi, wv_lo = sem("wv_in"), sem("wv_hi"), sem("wv_lo")
        qk_full, qk_hi, qk_lo, dup_in = sem("qk_full"), sem("qk_hi"), sem("qk_lo"), sem("dup_in")
        v_full, vt_ready, turn_full, v_hi, v_lo = sem("v_full"), sem("vt_ready"), sem("turn_full"), sem("v_hi"), sem("v_lo")
        mx_full, mx_free = sem("mx_full"), [sem("mx_free0"), sem("mx_free1")]
        nm_ready, nm_full, nm_t_ready = sem("nm_ready"), sem("nm_full"), sem("nm_t_ready")
        row_in = [sem(f"row_in{q}") for q in range(NT)]
        s_ready, e_ready, ph_ready, pl_ready = sem("s_ready"), sem("e_ready"), sem("ph_ready"), sem("pl_ready")
        acc_step, acc_ready, pv_done = sem("acc_step"), sem("acc_ready"), sem("pv_done")
        fold_full = sem("fold_full")
        ot_ready, rden_ready, o_ready, o_out = sem("ot_ready"), sem("rden_ready"), sem("o_ready"), [sem("o_out0"), sem("o_out1")]
        ob_in = [sem(f"ob_in{t}") for t in range(NT)]
        wo_in, wo_hi, wo_lo = sem("wo_in"), sem("wo_hi"), sem("wo_lo")
        bn2_done, mv2_done, ve2_ready, std2_ready, inv2_ready = (sem("bn2_done"), sem("mv2_done"), sem("ve2_ready"),
                                                                 sem("std2_ready"), sem("inv2_ready"))
        on_ready, tr_ready, aff_ready, onh_ready, onl_ready = (sem("on_ready"), sem("tr_ready"), sem("aff_ready"),
                                                               sem("onh_ready"), sem("onl_ready"))
        po_ready, y_ready = sem("po_ready"), sem("y_ready")
        z_in = [sem(f"z_in{i}") for i in range(4)]
        y_out = [sem(f"y_out{i}") for i in range(4)]

        block = ctx.enter_context(nc.Block())

        @block.sync
        def _(sp):
            with nc.allow_non_contiguous_dma(reason="per-channel parameters"):
                for i, v in enumerate((gamma1, beta1, gamma2, beta2, b_out)):
                    sp.dma_start(par[:, i, :], v.rearrange("(k p) -> p k", p=P)).then_inc(par_in, 16)

            def load_qk_weights(b_h, h):
                sp.wait_ge(qk_lo, h * NT)
                sp.wait_ge(wq_lo, h)
                for i in range(2):
                    col = b_h * DH + i * C
                    sp.dma_start(wq_raw[:, :, i * DH:(i + 1) * DH], w_v[:, :, bass.ds(col, DH)]).then_inc(wq_in, 16)
                    sp.dma_start(b_qk[i * DH:(i + 1) * DH, :],
                                 b_qkv[bass.ds(col, DH)].rearrange("(p o) -> p o", o=1)).then_inc(wq_in, 16)

            def load_v_weights(b_p, pair):
                sp.wait_ge(vt_ready, pair * NT)
                sp.wait_ge(wv_lo, pair)
                col = b_p * P + 2 * C
                sp.dma_start(wv_raw[:, :, :], w_v[:, :, bass.ds(col, P)]).then_inc(wv_in, 16)
                sp.dma_start(b_v[:, :], b_qkv[bass.ds(col, P)].rearrange("(p o) -> p o", o=1)).then_inc(wv_in, 16)

            def duplicate(h, s, t):
                sp.wait_ge(qk_hi, h * NT + t + 1)
                w = slice(t * W, (t + 1) * W)
                sp.dma_start(q_hh[s][DH:P, w].bitcast(F32), q_hh[s][0:DH, w].bitcast(F32)).then_inc(dup_in, 16)
                sp.dma_start(k_h1[s][0:DH, w].bitcast(F32), k_hl[s][0:DH, w].bitcast(F32)).then_inc(dup_in, 16)

            def max_row(h, s, q):
                sp.wait_ge(nm_t_ready, h * NT + q + 1)
                sp.dma_start(q_lm[s][DH:DH + 1, q * W:(q + 1) * W].bitcast(F32).rearrange("o (a b) -> o a b", a=4),
                             nm_t[:, q % 2, :].bitcast(F32)).then_inc(row_in[q], 16)

            def store_heads(b, b_h, h, q):
                sp.wait_ge(o_ready, h * NT + q + 1)
                sp.dma_start(o_v[bass.ds(b, 1), :, q * 4:(q + 1) * 4, bass.ds(b_h * DH, DH)].rearrange("o p t c -> (o p) t c"),
                             o_st[:, q % 2, :, :]).then_inc(o_out[q % 2], 16)

            def beside(b, p, slot, u):
                s, b_h = slot.odd, p * 2 + slot.odd
                if u in FOLD and not (slot.first and u == LAG):
                    q = FOLD[u]
                    store_heads(b, b_h + (-1 if q < 0 else 0), slot.h + (-1 if q < 0 else 0), q % NT)
                if u == LOAD_WEIGHTS and slot.has_pair:
                    load_qk_weights(b_h + 2, slot.h + 2)
                    if not slot.odd:
                        load_v_weights(p + 1, slot.pair + 1)
                t = ended(QK_PROJ, u)
                if t is not None and slot.has_next:
                    duplicate(slot.h + 1, 1 - s, t)
                if u in NM_TURN:
                    ahead, q = divmod(NM_TURN[u], NT)
                    if not ahead or slot.has_next:
                        max_row(slot.h + ahead, s ^ ahead, q)

            with sp.Fori(0, BATCH) as b:
                sp.wait_ge(pv_done, b * HEADS * UNITS)
                for k in range(NK):
                    sp.dma_start(xb[:, k, :], x_v[bass.ds(b, 1), :, k, :].rearrange("o p t -> (o p) t")).then_inc(x_in[k], 16)
                load_qk_weights(0, b * HEADS)
                load_v_weights(0, b * (HEADS // 2))
                for t in range(NT):
                    w = slice(t * W, (t + 1) * W)
                    sp.wait_ge(z_ready, b * NT + t + 1)
                    sp.dma_start(z_dram[bass.ds(b, 1), :, :, w].rearrange("o p k t -> (o p) k t"), xb[:, :, w]).then_inc(z_out, 16)
                for t in range(NT):
                    duplicate(b * HEADS, 0, t)
                load_qk_weights(1, b * HEADS + 1)
                max_row(b * HEADS, 0, 0)
                for slot, u in opening(b):
                    beside(b, 0, slot, u)
                with sp.Fori(0, HEADS // 2 - 1) as p:
                    for i, (slot, u) in enumerate(turn(b, p)):
                        beside(b, p if i < 2 * UNITS - OPEN else p + 1, slot, u)
                for slot, u in turn(b, HEADS // 2 - 1, last_pair=True):
                    beside(b, HEADS // 2 - 1, slot, u)
                store_heads(b, HEADS - 1, b * HEADS + (HEADS - 1), NT - 1)
                sp.wait_ge(z_out, b * (16 * NT) + 16 * NT)
                sp.wait_ge(pv_done, b * (HEADS * UNITS) + HEADS * UNITS)
                sp.wait_ge(acc_ready, b * (HEADS * UNITS) + HEADS * UNITS)
                sp.wait_ge(pl_ready, b * (HEADS * UNITS) + HEADS * UNITS)
                sp.dma_start(wo_raw, wo_v).then_inc(wo_in, 16)
                for i in range(2):
                    sp.wait_ge(o_out[i], (b + 1) * (16 * HEADS * NT // 2))
                for t in range(NT):
                    sp.dma_start(ob[:, t * 4:(t + 1) * 4, :],
                                 o_v[bass.ds(b, 1), :, t * 4:(t + 1) * 4, :].rearrange("o p t c -> (o p) t c")).then_inc(ob_in[t], 16)

                def store_y(t, c):
                    n = t * NK + c
                    sp.wait_ge(y_ready, b * (NT * NK) + n + 1)
                    sp.dma_start(out_v[bass.ds(b, 1), :, c, t * W:(t + 1) * W].rearrange("o p t -> (o p) t"),
                                 z_st[:, n % 4, :]).then_inc(y_out[n % 4], 16)

                for t in range(NT):
                    for c in range(NK):
                        if t > 0:
                            store_y(t - 1, c)
                        sp.wait_ge(y_out[c], b * (16 * NT) + 16 * t)
                        sp.dma_start(z_st[:, c, :],
                                     z_dram[bass.ds(b, 1), :, c, t * W:(t + 1) * W].rearrange("o p t -> (o p) t")).then_inc(z_in[c], 16)
                for c in range(NK):
                    store_y(NT - 1, c)
            for c in range(NK):
                sp.wait_ge(y_out[c], BATCH * 16 * NT)

        @block.gpsimd
        def _(pool):
            for tile, value in ((ident, 0.0), (zero, 0.0), (ones, 1.0), (avg_c, 1.0 / C), (avg_g, 1.0 / GROUP)):
                nc.gpsimd.memset(tile[:, :], value).then_inc(const_set, 1)
            pool.wait_ge(const_set, 5)
            nc.gpsimd.affine_select(out=ident[:, :], in_=ident[:, :], compare_op=ALU.not_equal, fill=1.0, base=0,
                                    pattern=[[-1, P]], channel_multiplier=1).then_inc(const_ready, 1)
            groups = avg_g[:, :].rearrange("p (g i) -> p g i", i=GROUP)
            nc.gpsimd.affine_select(out=groups, in_=groups, compare_op=ALU.is_ge, fill=0.0, base=0,
                                    pattern=[[-GROUP, P // GROUP], [0, GROUP]], channel_multiplier=1).then_inc(const_set, 1)
            pool.wait_ge(const_set, 6)
            nc.gpsimd.affine_select(out=groups, in_=groups, compare_op=ALU.is_ge, fill=0.0, base=GROUP - 1,
                                    pattern=[[GROUP, P // GROUP], [0, GROUP]], channel_multiplier=-1).then_inc(const_ready, 1)

            def unit(slot, u):
                q, j = divmod(u, UPB)
                pool.wait_ge(e_ready, slot.units * 2 + (2 * u + 2))
                two = [probs[:, u % 2, i * W:(i + 1) * W] for i in range(2)]
                if j == 0:
                    if q > 1 or not slot.first:
                        pool.wait_ge(fold_full, slot.h * NT + (q - 1))
                    nc.gpsimd.tensor_tensor(acc[:, q % 2, :], two[0], two[1], ALU.add).then_inc(acc_ready, 1)
                else:
                    pool.wait_ge(acc_ready, slot.units + u)
                    nc.gpsimd.tensor_tensor(acc[:, q % 2, :], acc[:, q % 2, :], two[0], ALU.add).then_inc(acc_step, 1)
                    pool.wait_ge(acc_step, slot.h * (UNITS - NT) + (u - q))
                    nc.gpsimd.tensor_tensor(acc[:, q % 2, :], acc[:, q % 2, :], two[1], ALU.add).then_inc(acc_ready, 1)

            with pool.Fori(0, BATCH) as b:
                for t in range(NT):
                    w = slice(t * W, (t + 1) * W)
                    pool.wait_ge(xn_ready, b * NT + t + 1)
                    nc.gpsimd.tensor_tensor(xb[:, :, w], xb[:, :, w], gb[:, :, w], ALU.add).then_inc(z_ready, 1)
                pool.wait_ge(z_out, (b + 1) * (16 * NT))
                pool.wait_ge(xl_ready, (b + 1) * NT)
                for s in range(2):
                    zeros, one = (c[DH:P, 0:1].to_broadcast([P - DH, T]) for c in (zero, ones))
                    nc.gpsimd.tensor_tensor(k_h1[s][DH:P, :], one, zeros, ALU.add).then_inc(rows_set, 1)
                    nc.gpsimd.tensor_tensor(q_lm[s][DH:P, :], zeros, zeros, ALU.add).then_inc(rows_set, 1)
                for slot, u in opening(b):
                    unit(slot, u)
                with pool.Fori(0, HEADS // 2 - 1) as p:
                    for slot, u in turn(b, p):
                        unit(slot, u)
                for slot, u in turn(b, HEADS // 2 - 1, last_pair=True):
                    unit(slot, u)

        @block.scalar
        def _(act):
            def split_qk(h):
                act.wait_ge(wq_in, h * 64 + 64)
                act.wait_ge(qk_full, h * NT)
                nc.scalar.activation(wq_h[:, :, :], wq_raw[:, :, :], ACT.Copy).then_inc(wq_hi, 1)

            def split_v(pair):
                act.wait_ge(wv_in, pair * 32 + 32)
                act.wait_ge(v_full, pair * NT)
                nc.scalar.activation(wv_h[:, :, :], wv_raw[:, :, :], ACT.Copy).then_inc(wv_hi, 1)

            def qk_halves(h, s, t, free):
                act.wait_ge(pv_done, free)
                act.wait_ge(qk_full, h * NT + (t + 1))
                w = slice(t * W, (t + 1) * W)
                nc.scalar.activation(q_hh[s][0:DH, w], ps[0:DH, BANK_PROJ, :], ACT.Identity, bias=b_qk[0:DH, :])
                nc.scalar.activation(k_hl[s][0:DH, w], ps[DH:P, BANK_PROJ, :], ACT.Identity,
                                     bias=b_qk[DH:P, :]).then_inc(qk_hi, 1)

            def v_rows(pair, t):
                act.wait_ge(v_full, pair * NT + (t + 1))
                nc.scalar.activation(vt[:, t * W:(t + 1) * W], ps[:, BANK_PROJ, :], ACT.Identity,
                                     bias=b_v[:, :]).then_inc(vt_ready, 1)

            def v_halves(h, s, t, free):
                act.wait_ge(turn_full, h * NT + (t + 1))
                act.wait_ge(pv_done, free)
                src = ps[:, BANK_PROJ, :].rearrange("p (t c) -> p t c", c=P)[:, :, s * DH:(s + 1) * DH]
                nc.scalar.activation(v_hl[:, s, t * 4:(t + 1) * 4, 0:DH], src, ACT.Copy).then_inc(v_hi, 1)

            def max_columns(h, q):
                act.wait_ge(nm_full, h * NT + (q + 1))
                act.wait_ge(row_in[(q + 2) % NT], h * 16 if q < 2 else h * 16 + 16)
                nc.scalar.activation(nm_t[:, q % 2, :], ps[0:4, BANK_MISC, 0:P], ACT.Copy).then_inc(nm_t_ready, 1)

            def take_output(slot, q):
                act.wait_ge(pv_done, slot.units + (q + 1) * UPB)
                act.wait_ge(fold_full, slot.h * NT + q)
                nc.scalar.activation(ot[:, :], ps[:, BANK_PV, :], ACT.Copy).then_inc(ot_ready, 1)

            def unit(slot, u):
                s = slot.odd
                if u in FOLD and not (slot.first and u == LAG):
                    take_output(slot, FOLD[u])
                t = ended(QK_PROJ, u)
                if t is not None and slot.has_next:
                    qk_halves(slot.h + 1, 1 - s, t, slot.units)
                t = ended(V_PROJ, u)
                if t is not None and slot.has_pair and slot.odd:
                    v_rows(slot.pair + 1, t)
                if u - 1 in V_TURN[slot.odd] and slot.has_next:
                    v_halves(slot.h + 1, 1 - s, V_TURN[slot.odd][u - 1], slot.units)
                if u - 1 in NM_TURN:
                    ahead, q = divmod(NM_TURN[u - 1], NT)
                    if not ahead or slot.has_next:
                        max_columns(slot.h + ahead, q)
                if u == SPLIT_QK and slot.has_pair:
                    split_qk(slot.h + 2)
                if u == SPLIT_V and slot.has_pair and not slot.odd:
                    split_v(slot.pair + 1)
                act.wait_ge(pl_ready, slot.two_before(u))
                act.wait_ge(acc_ready, slot.two_before(u))
                for i in range(2):
                    act.wait_ge(s_ready, slot.units * 2 + (2 * u + i + 1))
                    e = nc.scalar.activation(probs[:, u % 2, i * W:(i + 1) * W], ps[:, BANK_S[(2 * u + i + 64 * s) % 3], :],
                                             ACT.Exp, scale=SCALE).then_inc(e_ready, 1)
                act.wait_ge(e_ready, slot.units * 2 + (2 * u + 2))
                act.wait_ge(pv_done, slot.two_before(u))
                nc.scalar.activation(ph[:, u % 2, :], probs[:, u % 2, :], ACT.Copy).then_inc(ph_ready, 1)

            act.wait_ge(par_in, 80)
            with act.Fori(0, BATCH) as b:
                act.wait_ge(gn_dve, b * 4 + 3)
                nc.scalar.activation(gs[:, :], gv[:, :], ACT.Sqrt).then_inc(gn_std, 1)
                for t in range(NT):
                    act.wait_ge(dev_ready, b * NT + t + 1)
                    if t:
                        act.wait_ge(var_ready, b * NT + t)
                    nc.scalar.activation(sq, gb[:, :, t * W:(t + 1) * W], ACT.Square).then_inc(sq_ready, 1)
                for t in range(NT):
                    act.wait_ge(veps_ready, b * NT + t + 1)
                    nc.scalar.activation(inv[t], inv[t], ACT.Sqrt).then_inc(std_ready, 1)
                for t in range(NT):
                    act.wait_ge(norm_ready, b * NT + t + 1)
                    for k in range(NK):
                        w = gb[:, k, t * W:(t + 1) * W]
                        xn = nc.scalar.activation(w, w, ACT.Identity, scale=par[:, 0, k:k + 1], bias=par[:, 1, k:k + 1])
                    xn.then_inc(xn_ready, 1)
                split_qk(b * HEADS)
                split_v(b * (HEADS // 2))
                act.wait_ge(z_out, (b + 1) * (16 * NT))
                act.wait_ge(xl_ready, (b + 1) * NT)
                for t in range(NT):
                    qk_halves(b * HEADS, 0, t, b * (HEADS * UNITS))
                for c in range(NK):
                    act.wait_ge(y_out[c], b * (16 * NT))
                for t in range(NT):
                    v_rows(b * (HEADS // 2), t)
                for t in range(NT):
                    v_halves(b * HEADS, 0, t, b * (HEADS * UNITS))
                split_qk(b * HEADS + 1)
                max_columns(b * HEADS, 0)
                for slot, u in opening(b):
                    unit(slot, u)
                with act.Fori(0, HEADS // 2 - 1) as p:
                    for slot, u in turn(b, p):
                        unit(slot, u)
                for slot, u in turn(b, HEADS // 2 - 1, last_pair=True):
                    unit(slot, u)
                take_output(Slot(b + 1, 0, 0), -1)
                act.wait_ge(wo_in, (b + 1) * 16)
                nc.scalar.activation(wo_h, wo_raw, ACT.Copy).then_inc(wo_hi, 1)
                for t in range(NT):
                    act.wait_ge(ve2_ready, b * NT + t + 1)
                    nc.scalar.activation(rs2[:, t * 4:(t + 1) * 4], rs2[:, t * 4:(t + 1) * 4], ACT.Sqrt).then_inc(std2_ready, 1)
                for t in range(NT):
                    for k in range(NK):
                        n = t * NK + k
                        act.wait_ge(tr_ready, b * (NT * NK) + n + 1)
                        if n >= 4:
                            act.wait_ge(onl_ready, b * (NT * NK) + n - 3)
                        else:
                            act.wait_ge(fold_full, (b + 1) * (HEADS * NT))
                        nc.scalar.activation(on_st[n % 4], ps[:, n % 4, :], ACT.Identity, scale=par[:, 2, k:k + 1],
                                             bias=par[:, 3, k:k + 1]).then_inc(aff_ready, 1)
                        act.wait_ge(aff_ready, b * (NT * NK) + n + 1)
                        nc.scalar.activation(xh[:, k, t * W:(t + 1) * W], on_st[n % 4], ACT.Copy).then_inc(onh_ready, 1)

        @block.vector
        def _(dve):
            def split_qk(h):
                dve.wait_ge(wq_hi, h + 1)
                nc.vector.tensor_tensor(wq_l[:, :, :], wq_raw[:, :, :], wq_h[:, :, :], ALU.subtract).then_inc(wq_lo, 1)

            def split_v(pair):
                dve.wait_ge(wv_hi, pair + 1)
                nc.vector.tensor_tensor(wv_l[:, :, :], wv_raw[:, :, :], wv_h[:, :, :], ALU.subtract).then_inc(wv_lo, 1)

            def qk_remainders(h, s, t):
                dve.wait_ge(qk_hi, h * NT + t + 1)
                w = slice(t * W, (t + 1) * W)
                nc.vector.scalar_tensor_tensor(out=q_lm[s][0:DH, w], in0=ps[0:DH, BANK_PROJ, :], scalar=b_qk[0:DH, :],
                                               in1=q_hh[s][0:DH, w], op0=ALU.add, op1=ALU.subtract)
                nc.vector.scalar_tensor_tensor(out=k_hl[s][DH:P, w], in0=ps[DH:P, BANK_PROJ, :], scalar=b_qk[DH:P, :],
                                               in1=k_hl[s][0:DH, w], op0=ALU.add, op1=ALU.subtract).then_inc(qk_lo, 1)

            def v_remainders(h, s, t):
                dve.wait_ge(v_hi, h * NT + t + 1)
                src = ps[:, BANK_PROJ, :].rearrange("p (t c) -> p t c", c=P)[:, :, s * DH:(s + 1) * DH]
                nc.vector.tensor_tensor(v_hl[:, s, t * 4:(t + 1) * 4, DH:P], src, v_hl[:, s, t * 4:(t + 1) * 4, 0:DH],
                                        ALU.subtract).then_inc(v_lo, 1)

            def reduce_max(h, q, step, base, half, n):
                dve.wait_ge(mx_full, base + (n + 1))
                i, kc = divmod(step, NT)
                nc.vector.tensor_reduce(nm4[:, q % 2, i, kc:kc + 1], ps[:, BANK_MX[n % 2], :], op=ALU.max, axis=AX.X,
                                        negate=True).then_inc(mx_free[n % 2], 1)
                if step == 4 * NT - 1:
                    for parity in range(2):
                        dve.wait_ge(mx_free[parity], half + (n + 2 - parity) // 2)
                    nc.vector.tensor_reduce(nm[:, q % 2, :], nm4[:, q % 2, :, :], op=ALU.min, axis=AX.X).then_inc(nm_ready, 1)

            def take_fold(h, q):
                dve.wait_ge(fold_full, h * NT + (q + 1))
                src = ps[:, BANK_MISC, 0:4 * (DH + 1)].rearrange("p (t c) -> p t c", c=DH + 1)
                nc.vector.reciprocal(rden[:, :], src[:, :, DH]).then_inc(rden_ready, 1)
                dve.wait_ge(rden_ready, h * NT + (q + 1))
                dve.wait_ge(o_out[q % 2], h * (16 * NT // 2) + 16 * (q // 2))
                nc.vector.tensor_tensor(o_st[:, q % 2, :, :], src[:, :, 0:DH],
                                        rden[:, :].rearrange("p (t o) -> p t o", o=1).to_broadcast([P, 4, DH]),
                                        ALU.mult).then_inc(o_ready, 1)

            def unit(slot, u):
                s = slot.odd
                if u - 1 in FOLD and not (slot.first and u - 1 == LAG):
                    q = FOLD[u - 1]
                    take_fold(slot.h + (-1 if q < 0 else 0), q % NT)
                t = ended(QK_PROJ, u)
                if t is not None and slot.has_next:
                    qk_remainders(slot.h + 1, 1 - s, t)
                if u - 1 in V_TURN[slot.odd] and slot.has_next:
                    v_remainders(slot.h + 1, 1 - s, V_TURN[slot.odd][u - 1])
                if u == SPLIT_QK and slot.has_pair:
                    split_qk(slot.h + 2)
                if u == SPLIT_V and slot.has_pair and not slot.odd:
                    split_v(slot.pair + 1)
                for i, (ahead, q, step) in enumerate(max_steps(slot, u)):
                    reduce_max(slot.h + ahead, q, step, slot.mx, slot.mx_half, 2 * u + i)
                dve.wait_ge(ph_ready, slot.units + (u + 1))
                dve.wait_ge(pv_done, slot.two_before(u))
                nc.vector.tensor_tensor(pl[:, u % 2, :], probs[:, u % 2, :], ph[:, u % 2, :],
                                        ALU.subtract).then_inc(pl_ready, 1)

            dve.wait_ge(par_in, 80)
            dve.wait_ge(const_ready, 1)
            nc.vector.tensor_tensor(fold[:, :], ident[:, 0:DH], ident[:, DH:P], ALU.add).then_inc(fold_ready, 1)
            with dve.Fori(0, BATCH) as b:
                for k in range(NK):
                    dve.wait_ge(x_in[k], b * 16 + 16)
                    for t in range(NT):
                        nc.vector.bn_stats(bn[:, k, t, :], xb[:, k, t * W:(t + 1) * W]).then_inc(bn_done, 1)
                dve.wait_ge(bn_done, (b + 1) * (NK * NT))
                nc.vector.memset(carrier[:, :], 0.0)
                for k in range(NK):
                    nc.vector.bn_aggr(mv[:, k, :], bn[:, k, :, :]).then_inc(gn_in if k == NK - 1 else bn_agg, 1)
                dve.wait_ge(gn_sum, b * 2 + 1)
                nc.vector.tensor_copy(gm[:, :], ps[:, BANK_MISC, 0:NK]).then_inc(gn_dve, 1)
                dve.wait_ge(gn_dve, b * 4 + 1)
                nc.vector.tensor_tensor(gv[:, :], mv[:, :, 0], gm[:, :], ALU.subtract).then_inc(bn_agg, 1)
                dve.wait_ge(bn_agg, (b + 1) * (NK + 1) - 1)
                nc.vector.tensor_tensor(gv[:, :], gv[:, :], gv[:, :], ALU.mult).then_inc(bn_agg, 1)
                dve.wait_ge(bn_agg, (b + 1) * (NK + 1))
                nc.vector.tensor_tensor(gs[:, :], gv[:, :], mv[:, :, 1], ALU.add).then_inc(gn_dve, 1)
                dve.wait_ge(gn_sum, b * 2 + 2)
                nc.vector.tensor_scalar(gv[:, :], ps[:, BANK_MISC, 0:NK], EPS, None, ALU.add).then_inc(gn_dve, 1)
                dve.wait_ge(gn_std, b + 1)
                nc.vector.reciprocal(gs[:, :], gs[:, :]).then_inc(gn_dve, 1)
                dve.wait_ge(gn_dve, b * 4 + 4)
                for k in range(NK):
                    nc.vector.tensor_scalar(gb[:, k, :], xb[:, k, :], gm[:, k:k + 1], gs[:, k:k + 1], ALU.subtract,
                                            ALU.mult).then_inc(g_ready, 1)
                dve.wait_ge(g_ready, (b + 1) * NK)
                for t in range(NT):
                    dve.wait_ge(mean_ready, b * NT + t + 1)
                    w = gb[:, :, t * W:(t + 1) * W]
                    mean = ps[:, t:t + 1, :].to_broadcast([P, NK, W])
                    nc.vector.tensor_tensor(w, w, mean, ALU.subtract).then_inc(dev_ready, 1)
                for t in range(NT):
                    dve.wait_ge(var_ready, b * NT + t + 1)
                    nc.vector.tensor_scalar(inv[t], ps[:, 4 + t, :], EPS, None, ALU.add).then_inc(veps_ready, 1)
                for t in range(NT):
                    dve.wait_ge(std_ready, b * NT + t + 1)
                    nc.vector.reciprocal(inv[t], inv[t]).then_inc(inv_ready, 1)
                    dve.wait_ge(inv_ready, b * NT + t + 1)
                    w = gb[:, :, t * W:(t + 1) * W]
                    nc.vector.tensor_tensor(w, w, inv[t].rearrange("p (o w) -> p o w", o=1).to_broadcast([P, NK, W]),
                                            ALU.mult).then_inc(norm_ready, 1)
                for t in range(NT):
                    w = slice(t * W, (t + 1) * W)
                    dve.wait_ge(xn_ready, b * NT + t + 1)
                    nc.vector.tensor_copy(xh[:, :, w], gb[:, :, w]).then_inc(xh_ready, 1)
                    dve.wait_ge(xh_ready, b * NT + t + 1)
                    nc.vector.tensor_tensor(xl[:, :, w], gb[:, :, w], xh[:, :, w], ALU.subtract).then_inc(xl_ready, 1)
                split_qk(b * HEADS)
                split_v(b * (HEADS // 2))
                dve.wait_ge(z_out, (b + 1) * (16 * NT))
                dve.wait_ge(xl_ready, (b + 1) * NT)
                for t in range(NT):
                    qk_remainders(b * HEADS, 0, t)
                for t in range(NT):
                    v_remainders(b * HEADS, 0, t)
                split_qk(b * HEADS + 1)
                for n in range(PRO_MX):
                    q, step = divmod(n, 16)
                    reduce_max(b * HEADS, q, step, b * BATCH_MX, b * (BATCH_MX // 2), n)
                for slot, u in opening(b):
                    unit(slot, u)
                with dve.Fori(0, HEADS // 2 - 1) as p:
                    for slot, u in turn(b, p):
                        unit(slot, u)
                for slot, u in turn(b, HEADS // 2 - 1, last_pair=True):
                    unit(slot, u)
                take_fold(b * HEADS + (HEADS - 1), NT - 1)
                dve.wait_ge(wo_hi, b + 1)
                nc.vector.tensor_tensor(wo_l, wo_raw, wo_h, ALU.subtract).then_inc(wo_lo, 1)
                for t in range(NT):
                    dve.wait_ge(ob_in[t], b * 16 + 16)
                    for i in range(4 * t, 4 * t + 4):
                        nc.vector.bn_stats(bn2[:, i, :], ob[:, i, :]).then_inc(bn2_done, 1)
                    dve.wait_ge(bn2_done, b * KB + 4 * t + 4)
                    nc.vector.memset(carrier[:, :], 0.0)
                    for i in range(4 * t, 4 * t + 4):
                        nc.vector.bn_aggr(mv2[:, i, :], bn2[:, i, :]).then_inc(mv2_done, 1)
                    dve.wait_ge(mv2_done, b * KB + 4 * t + 4)
                    nc.vector.tensor_scalar(rs2[:, 4 * t:4 * t + 4], mv2[:, 4 * t:4 * t + 4, 1], EPS, None,
                                            ALU.add).then_inc(ve2_ready, 1)
                for t in range(NT):
                    r = rs2[:, 4 * t:4 * t + 4]
                    dve.wait_ge(std2_ready, b * NT + t + 1)
                    nc.vector.reciprocal(r, r).then_inc(inv2_ready, 1)
                    dve.wait_ge(inv2_ready, b * NT + t + 1)
                    for i in range(4 * t, 4 * t + 4):
                        on = nc.vector.tensor_scalar(ob[:, i, :], ob[:, i, :], mv2[:, i, 0:1], rs2[:, i:i + 1],
                                                     ALU.subtract, ALU.mult)
                    on.then_inc(on_ready, 1)

                def remainders(t):
                    for k in range(NK):
                        n = t * NK + k
                        dve.wait_ge(onh_ready, b * (NT * NK) + n + 1)
                        nc.vector.tensor_tensor(xl[:, k, t * W:(t + 1) * W], on_st[n % 4], xh[:, k, t * W:(t + 1) * W],
                                                ALU.subtract).then_inc(onl_ready, 1)

                def residuals(t):
                    for c in range(NK):
                        n = t * NK + c
                        dve.wait_ge(po_ready, b * (NT * NK) + n + 1)
                        dve.wait_ge(z_in[c], b * (16 * NT) + 16 * (t + 1))
                        nc.vector.scalar_tensor_tensor(out=z_st[:, c, :], in0=ps[:, 4 + c, :], scalar=par[:, 4, c:c + 1],
                                                       in1=z_st[:, c, :], op0=ALU.add, op1=ALU.add).then_inc(y_ready, 1)

                remainders(0)
                for t in range(NT):
                    if t + 1 < NT:
                        remainders(t + 1)
                    residuals(t)

        @block.tensor
        def _(pe):
            def project(w_h, w_l, t, part, parts, full):
                w = slice(t * W, (t + 1) * W)
                terms = [(a, k, x) for k in range(NK) for a, x in ((w_h, xh), (w_l, xh), (w_h, xl))]
                n = len(terms) // parts
                for i, (a, k, x) in enumerate(terms[part * n:(part + 1) * n], part * n):
                    last = nc.tensor.matmul(ps[:, BANK_PROJ, :], a[:, k, :], x[:, k, w], start=(i == 0),
                                            stop=(i == len(terms) - 1))
                if part == parts - 1:
                    last.then_inc(full, 1)

            def turn_v(h, pair, t):
                pe.wait_ge(vt_ready, pair * NT + (t + 1))
                for i in range(4):
                    last = nc.tensor.transpose(ps[:, BANK_PROJ, i * P:(i + 1) * P],
                                               vt[:, t * W + i * P:t * W + (i + 1) * P], ident[:, :])
                last.then_inc(turn_full, 1)

            def scores_for_max(h, s, q, step, half, n):
                i, kc = divmod(step, NT)
                if step == 0 and q == 0:
                    pe.wait_ge(dup_in, h * (32 * NT) + 32 * NT)
                    pe.wait_ge(qk_lo, h * NT + NT)
                pe.wait_ge(mx_free[n % 2], half + n // 2)
                qs = q * W + i * P
                nc.tensor.matmul(ps[:, BANK_MX[n % 2], :], q_hh[s][:, qs:qs + P], k_hl[s][:, kc * W:(kc + 1) * W],
                                 start=True, stop=True).then_inc(mx_full, 1)

            def turn_max(h, q):
                pe.wait_ge(nm_ready, h * NT + (q + 1))
                nc.tensor.matmul(ps[0:4, BANK_MISC, 0:P], nm[:, q % 2, :], ident[:, :], start=True, stop=True).then_inc(nm_full, 1)

            def fold_output(slot, q):
                pe.wait_ge(ot_ready, slot.h * NT + (q + 1))
                pe.wait_ge(acc_ready, slot.units + (q + 1) * UPB)
                for i in range(4):
                    o, w = i * (DH + 1), slice(i * P, (i + 1) * P)
                    nc.tensor.matmul(ps[:, BANK_MISC, o:o + DH], ot[:, w], fold[:, :], start=True, stop=True)
                    last = nc.tensor.matmul(ps[:, BANK_MISC, o + DH:o + DH + 1], acc[:, q % 2, w], ones[:, :],
                                            start=True, stop=True)
                last.then_inc(fold_full, 1)

            def probs_times_v(slot, u):
                q, j = divmod(u, UPB)
                s = slot.odd if u >= 0 else 1 - slot.odd
                pe.wait_ge(pl_ready, slot.units + (u + 1))
                if j == 0:
                    if u == 0:
                        pe.wait_ge(v_lo, slot.h * NT + NT)
                    if u or not slot.first:
                        pe.wait_ge(ot_ready, slot.h * NT + q)
                for i in range(2):
                    v = v_hl[:, s, 2 * j + i, :]
                    nc.tensor.matmul(ps[:, BANK_PV, :], v, ph[:, u % 2, i * W:(i + 1) * W], start=(j == 0 and i == 0), stop=False)
                    last = nc.tensor.matmul(ps[:, BANK_PV, :], v, pl[:, u % 2, i * W:(i + 1) * W], start=False,
                                            stop=(j == UPB - 1 and i == 1))
                last.then_inc(pv_done, 1)

            def scores(slot, u):
                q, j = divmod(u, UPB)
                s = slot.odd
                if j == 0:
                    pe.wait_ge(row_in[q], slot.h * 16 + 16)
                w = slice(q * W, (q + 1) * W)
                for i in range(2):
                    n = 2 * u + i
                    if n > 2 or not slot.first:
                        back = 1 if n < 2 and not s else 2
                        pe.wait_ge(e_ready, slot.units * 2 + (n - back))
                    k = slice((2 * j + i) * P, (2 * j + i + 1) * P)
                    bank = BANK_S[(n + 64 * s) % 3]
                    nc.tensor.matmul(ps[:, bank, :], k_hl[s][:, k], q_hh[s][:, w], start=True, stop=False)
                    nc.tensor.matmul(ps[:, bank, :], k_h1[s][:, k], q_lm[s][:, w], start=False, stop=True).then_inc(s_ready, 1)

            def unit(slot, u):
                s = slot.odd
                scores(slot, u)
                if u >= LAG or not slot.first:
                    probs_times_v(slot, u - LAG)
                for i, (ahead, q, step) in enumerate(max_steps(slot, u)):
                    scores_for_max(slot.h + ahead, s ^ ahead, q, step, slot.mx_half, 2 * u + i)
                if u in QK_PROJ and slot.has_next:
                    t, part, parts = QK_PROJ[u]
                    if u == 0:
                        pe.wait_ge(v_lo, slot.h * NT + NT)
                        pe.wait_ge(wq_lo, slot.h + 2)
                    elif part == 0:
                        pe.wait_ge(qk_lo, slot.h * NT + (NT + t))
                    project(wq_h, wq_l, t, part, parts, qk_full)
                if u in V_PROJ and slot.odd and slot.has_pair:
                    t, part, parts = V_PROJ[u]
                    if part == 0:
                        if t == 0:
                            pe.wait_ge(qk_lo, slot.h * NT + 2 * NT)
                            pe.wait_ge(wv_lo, slot.pair + 2)
                        else:
                            pe.wait_ge(vt_ready, slot.pair * NT + (NT + t))
                    project(wv_h, wv_l, t, part, parts, v_full)
                if u in V_TURN[slot.odd] and slot.has_next:
                    t = V_TURN[slot.odd][u]
                    if t:
                        pe.wait_ge(v_lo, slot.h * NT + (NT + t))
                    elif not slot.odd:
                        pe.wait_ge(qk_lo, slot.h * NT + 2 * NT)
                    else:
                        pe.wait_ge(vt_ready, slot.pair * NT + 2 * NT)
                    turn_v(slot.h + 1, slot.pair + slot.odd, t)
                if u in NM_TURN:
                    ahead, q = divmod(NM_TURN[u], NT)
                    if not ahead or slot.has_next:
                        if u > AHEAD or not slot.first:
                            pe.wait_ge(o_ready, slot.h * NT + q_folded(u))
                        turn_max(slot.h + ahead, q)
                if u in FOLD and not (slot.first and u == LAG):
                    q = FOLD[u]
                    pe.wait_ge(nm_t_ready, slot.h * NT + (q + 2))
                    fold_output(slot, q)

            def q_folded(u):
                return sum(1 for v, q in FOLD.items() if v < u and q >= 0)

            pe.wait_ge(const_ready, 2)
            pe.wait_ge(fold_ready, 1)
            with pe.Fori(0, BATCH) as b:
                pe.wait_ge(y_ready, b * (NT * NK))
                pe.wait_ge(onh_ready, b * (NT * NK))
                pe.wait_ge(gn_in, b + 1)
                pe.wait_ge(bn_agg, b * (NK + 1) + NK - 1)
                nc.tensor.matmul(ps[:, BANK_MISC, 0:NK], avg_g[:, :], mv[:, :, 0], start=True, stop=True).then_inc(gn_sum, 1)
                pe.wait_ge(gn_dve, b * 4 + 2)
                nc.tensor.matmul(ps[:, BANK_MISC, 0:NK], avg_g[:, :], gs[:, :], start=True, stop=True).then_inc(gn_sum, 1)
                pe.wait_ge(g_ready, (b + 1) * NK)
                for t in range(NT):
                    for k in range(NK):
                        last = nc.tensor.matmul(ps[:, t, :], avg_c[:, :], gb[:, k, t * W:(t + 1) * W], start=(k == 0), stop=(k == NK - 1))
                    last.then_inc(mean_ready, 1)
                for t in range(NT):
                    pe.wait_ge(sq_ready, b * NT + t + 1)
                    if t == NT - 1:
                        pe.wait_ge(gn_dve, b * 4 + 3)
                    for k in range(NK):
                        last = nc.tensor.matmul(ps[:, 4 + t, :], avg_c[:, :], sq[:, k, :], start=(k == 0), stop=(k == NK - 1))
                    last.then_inc(var_ready, 1)
                pe.wait_ge(veps_ready, (b + 1) * NT)
                pe.wait_ge(wq_lo, b * HEADS + 1)
                for t in range(NT):
                    pe.wait_ge(xl_ready, b * NT + t + 1)
                    if t:
                        pe.wait_ge(qk_lo, b * (HEADS * NT) + t)
                    project(wq_h, wq_l, t, 0, 1, qk_full)
                pe.wait_ge(wv_lo, b * (HEADS // 2) + 1)
                pe.wait_ge(qk_lo, b * (HEADS * NT) + NT)
                for t in range(NT):
                    if t:
                        pe.wait_ge(vt_ready, b * (HEADS // 2 * NT) + t)
                    project(wv_h, wv_l, t, 0, 1, v_full)
                pe.wait_ge(vt_ready, b * (HEADS // 2 * NT) + NT)
                for t in range(NT):
                    if t:
                        pe.wait_ge(v_lo, b * (HEADS * NT) + t)
                    turn_v(b * HEADS, b * (HEADS // 2), t)
                pe.wait_ge(rows_set, (b + 1) * 4)
                for n in range(PRO_MX):
                    q, step = divmod(n, 16)
                    scores_for_max(b * HEADS, 0, q, step, b * (BATCH_MX // 2), n)
                    if n == 15:
                        turn_max(b * HEADS, 0)
                for slot, u in opening(b):
                    unit(slot, u)
                with pe.Fori(0, HEADS // 2 - 1) as p:
                    for slot, u in turn(b, p):
                        unit(slot, u)
                for slot, u in turn(b, HEADS // 2 - 1, last_pair=True):
                    unit(slot, u)
                after = Slot(b + 1, 0, 0)
                for u in range(-LAG, 0):
                    probs_times_v(after, u)
                fold_output(after, -1)
                def turn_outputs(t):
                    pe.wait_ge(on_ready, b * NT + t + 1)
                    for k in range(NK):
                        n = t * NK + k
                        if n >= 4:
                            pe.wait_ge(aff_ready, b * (NT * NK) + n - 3)
                        for i in range(4):
                            last = nc.tensor.transpose(ps[:, n % 4, i * P:(i + 1) * P], ob[:, 4 * t + i, k * P:(k + 1) * P], ident[:, :])
                        last.then_inc(tr_ready, 1)

                pe.wait_ge(e_ready, (b + 1) * (2 * HEADS * UNITS))
                pe.wait_ge(o_ready, (b + 1) * (HEADS * NT))
                for parity in range(2):
                    pe.wait_ge(mx_free[parity], (b + 1) * (BATCH_MX // 2))
                turn_outputs(0)
                pe.wait_ge(wo_lo, b + 1)
                for t in range(NT):
                    if t + 1 < NT:
                        turn_outputs(t + 1)
                    pe.wait_ge(onl_ready, b * (NT * NK) + (t + 1) * NK)
                    w = slice(t * W, (t + 1) * W)
                    for c in range(NK):
                        if t > 0:
                            pe.wait_ge(y_ready, b * (NT * NK) + (t - 1) * NK + c + 1)
                        cs = slice(c * P, (c + 1) * P)
                        for k in range(NK):
                            nc.tensor.matmul(ps[:, 4 + c, :], wo_h[:, k, cs], xh[:, k, w], start=(k == 0), stop=False)
                            nc.tensor.matmul(ps[:, 4 + c, :], wo_l[:, k, cs], xh[:, k, w], start=False, stop=False)
                            last = nc.tensor.matmul(ps[:, 4 + c, :], wo_h[:, k, cs], xl[:, k, w], start=False, stop=(k == NK - 1))
                        last.then_inc(po_ready, 1)


_INS = ["x", "L0_conv_w_qkv", "L0_conv_b_qkv", "L0_conv_w_out", "L0_conv_b_out", "L0_conv_gamma1", "L0_conv_beta1",
        "L0_conv_gamma2", "L0_conv_beta2"]


def kernel(**inputs):
    import numpy as _np
    import concourse.bacc as _bacc
    from concourse import mybir as _mybir
    from concourse.bass_utils import run_bass_kernel_spmd as _run

    nc = _bacc.Bacc("TRN2", target_bir_lowering=False, num_devices=1)
    arrays, args = {}, []
    for name in _INS:
        a = _np.ascontiguousarray(inputs[name])
        arrays[f"in_{name}_dram"] = a
        args.append(nc.dram_tensor(f"in_{name}_dram", a.shape, _mybir.dt.from_np(a.dtype), kind="ExternalInput").ap())
    args.append(nc.dram_tensor("out_0_dram", (4, 512, 64, 32), _mybir.dt.float32, kind="ExternalOutput").ap())
    program(nc, *args)
    r = _run(nc, [arrays], core_ids=[0])
    return r.results[0]["out_0_dram"]
```

```python
import concourse.bass as bass
from concourse import mybir
from contextlib import ExitStack

F32 = mybir.dt.float32
F32R = mybir.dt.float32r
ALU = mybir.AluOpType
ACT = mybir.ActivationFunctionType
AX = mybir.AxisListType

P = 128
BATCH, C, T = 4, 512, 2048
HEADS = 8
DH = C // HEADS
SCALE = float(DH) ** -0.5
EPS = 1e-5
GROUP = C // 32
NK = C // P
W = 512
NT = T // W
KB = T // P
UPB = KB // 2
UNITS = NT * UPB
LAG = 2

BANK_S = [0, 1, 2]
BANK_PROJ = 3
BANK_MX = [4, 5]
BANK_PV = 6
BANK_MISC = 7

AHEAD = UPB // 2
QK_PROJ = {4 * t + i: (t, i, 3) for t in range(NT) for i in range(3)}
V_PROJ = {16 + 2 * t + i: (t, i, 2) for t in range(NT) for i in range(2)}
V_TURN = [{16 + 2 * t: t for t in range(NT)},
          {24 + 2 * t: t for t in range(NT)}]
LOAD_WEIGHTS, SPLIT_QK, SPLIT_V = 16, 21, 23
NM_TURN = {UPB * n + AHEAD: n + 1 for n in range(NT)}
FOLD = {UPB * n + LAG: n - 1 for n in range(NT)}
LOAD_WO, LOAD_OB, SPLIT_WO, LOAD_Z = 1, 5, 10, 14
OUT_STATS = {UPB * t + LAG + 10: t for t in range(NT - 1)}
OUT_NORM = 21
OUT_EARLY = 2
OUT_TURN = {OUT_NORM + 1 + n: divmod(n, NK) for n in range(OUT_EARLY * NK)}
BANK_TURN = BANK_PROJ
BANK_OUT = BANK_MX
OPEN = 4


def max_steps(slot, u):
    n, s = divmod(2 * (u + AHEAD), 4 * NT)
    return [(*divmod(n + 1, NT), s + i) for i in range(2)] if n + 1 < NT or slot.has_next else []


def ended(plan, u):
    t, part, parts = plan.get(u - 1, (0, 0, 2))
    return t if part == parts - 1 else None


PRO_MX = 24
PRO_TURN = {1 + 3 * t: t for t in range(NT)}
SLOT_MX = 4 * KB
BATCH_MX = SLOT_MX * HEADS


class Slot:

    def __init__(self, b, p, odd, last_pair=False, first=False):
        self.odd, self.first = odd, first
        self.has_next, self.has_pair = not (last_pair and odd), not last_pair
        self.h = b * HEADS + p * 2 + odd
        self.pair = b * (HEADS // 2) + p
        self.stores = (b * (HEADS - 1) + p * 2 + odd) * (16 * NT // 2)
        self.units = self.h * UNITS
        self.mx = b * BATCH_MX + p * (2 * SLOT_MX) + (PRO_MX + odd * SLOT_MX)
        self.mx_half = b * (BATCH_MX // 2) + p * SLOT_MX + (PRO_MX + odd * SLOT_MX) // 2

    def two_before(self, u):
        return self.units + (u - 1 if u > 1 or not self.first else 0)


def opening(b):
    return [(Slot(b, 0, 0, first=True), u) for u in range(OPEN)]


def turn(b, p, last_pair=False):
    even, odd = Slot(b, p, 0, last_pair, first=True), Slot(b, p, 1, last_pair)
    units = [(even, u) for u in range(OPEN, UNITS)] + [(odd, u) for u in range(UNITS)]
    return units + ([] if last_pair else [(Slot(b, p + 1, 0), u) for u in range(OPEN)])


def program(nc, x, w_qkv, b_qkv, w_out, b_out, gamma1, beta1, gamma2, beta2, out):
    x_v = x.rearrange("b (k p) f t -> b p k (f t)", p=P)
    out_v = out.rearrange("b (k p) f t -> b p k (f t)", p=P)
    w_v = w_qkv.rearrange("(k p) n -> p k n", p=P)
    wo_v = w_out.rearrange("(k p) n -> p k n", p=P)
    z_dram = nc.dram_tensor("z_scratch", (BATCH, P, NK, T), F32, kind="Internal").ap()
    o_dram = nc.dram_tensor("o_scratch", (BATCH, T, C), F32, kind="Internal").ap()
    o_v = o_dram.rearrange("b (t p) c -> b p t c", p=P)

    ctx = ExitStack()
    with ctx:
        def sb(name, shape, dt=F32):
            return ctx.enter_context(nc.sbuf_tensor(name, shape, dt))

        def sem(name):
            return ctx.enter_context(nc.semaphore(name))

        with ExitStack() as shared:
            gb = shared.enter_context(nc.sbuf_tensor("gb", [P, NK, T], F32))
            xb = shared.enter_context(nc.sbuf_tensor("xb", [P, NK, T], F32))
        with ExitStack() as shared:
            ob = shared.enter_context(nc.sbuf_tensor("ob", [P, KB, C], F32))
        k_hl, k_h1, q_hh, q_lm = [], [], [], []
        for s in range(2):
            k_hl.append(sb(f"k_hl{s}", [P, T], F32R))
            k_h1.append(sb(f"k_h1{s}", [P, T], F32R))
            q_hh.append(sb(f"q_hh{s}", [P, T], F32R))
            q_lm.append(sb(f"q_lm{s}", [P, T], F32R))
        xh = sb("xh", [P, NK, T], F32R)
        xl = sb("xl", [P, NK, T], F32R)
        v_hl = sb("v_hl", [P, 2, KB, P], F32R)
        vt = sb("vt", [P, T])
        probs = sb("probs", [P, 2, 2 * W])
        with ExitStack() as shared:
            sq1 = shared.enter_context(nc.sbuf_tensor("sq1", [P, NK, W], F32))
        ph = sb("ph", [P, 2, 2 * W], F32R)
        pl = sb("pl", [P, 2, 2 * W], F32R)
        acc = sb("acc", [P, 2, W])
        wq_raw = sb("wq_raw", [P, NK, P])
        w_halves = sb("w_halves", [P, 4, NK, P], F32R)
        wv_raw = sb("wv_raw", [P, NK, P])
        wq_h, wq_l, wv_h, wv_l = (w_halves[:, i, :, :] for i in range(4))
        b_qk = sb("b_qk", [P, 1])
        b_v = sb("b_v", [P, 1])
        ot = sb("ot", [P, W])
        rs = sb("rs", [P, 2, W])
        o_st = sb("o_st", [P, 2, 4, DH])
        nm4 = sb("nm4", [P, 2, 4, NT])
        nm = sb("nm", [P, 2, 4])
        nm_t = sb("nm_t", [4, 2, P], F32R)
        rden = sb("rden", [P, 4])
        carrier = sb("carrier", [P, 1])
        ident = sb("ident", [P, P])
        fold = sb("fold", [P, DH])
        ones = sb("ones", [P, 1])
        zero = sb("zero", [P, 1])
        avg_c = sb("avg_c", [P, P])
        avg_g = sb("avg_g", [P, P])
        par = sb("par", [P, 5, NK])
        bn = sb("bn", [P, NK, NT, 6])
        mv = sb("mv", [P, NK, 2])
        gm = sb("gm", [P, NK])
        gv = sb("gv", [P, NK])
        gs = sb("gs", [P, NK])
        rstd = sb("rstd", [P, KB])
        bn2 = sb("bn2", [P, KB, 6])
        mv2 = sb("mv2", [P, KB, 2])
        rs2 = sb("rs2", [P, KB])
        sq = [probs[:, :, :].rearrange("p a (k w) -> p (a k) w", w=W),
              sq1[:, :, :]]
        diag = [acc[:, 0, :], acc[:, 1, :], rs[:, 0, :], rs[:, 1, :]]
        on_st = [rs[:, 0, :], rs[:, 1, :]]
        wo_raw = vt[:, :].rearrange("p (k w) -> p k w", w=W)
        wo_h = v_hl[:, 0, :, :].rearrange("p t c -> p (t c)").rearrange("p (k w) -> p k w", w=W)
        wo_l = w_halves[:, :, :, :].rearrange("p a k c -> p a (k c)")
        z_st = vt[:, :].rearrange("p (k w) -> p k w", w=W)

        ps = ctx.enter_context(nc.psum_tensor("ps", [P, 8, W], F32))

        const_set, const_ready, fold_ready, par_in = sem("const_set"), sem("const_ready"), sem("fold_ready"), sem("par_in")
        x_in = [sem(f"x_in{k}") for k in range(NK)]
        bn_done, bn_agg = sem("bn_done"), sem("bn_agg")
        gn_in, gn_sum, gn_dve, gn_std = sem("gn_in"), sem("gn_sum"), sem("gn_dve"), sem("gn_std")
        g_ready, mean_ready, dev_ready, sq_ready = sem("g_ready"), sem("mean_ready"), sem("dev_ready"), sem("sq_ready")
        var_ready, veps_ready, std_ready, inv_ready = sem("var_ready"), sem("veps_ready"), sem("std_ready"), sem("inv_ready")
        diag_ready, spread_ready = sem("diag_ready"), sem("spread_ready")
        norm_ready, xn_ready, xh_ready, xl_ready = sem("norm_ready"), sem("xn_ready"), sem("xh_ready"), sem("xl_ready")
        z_ready, z_out, rows_set = sem("z_ready"), sem("z_out"), sem("rows_set")
        wq_in, wq_hi, wq_lo = sem("wq_in"), sem("wq_hi"), sem("wq_lo")
        wv_in, wv_hi, wv_lo = sem("wv_in"), sem("wv_hi"), sem("wv_lo")
        qk_full, qk_hi, qk_lo, dup_in = sem("qk_full"), sem("qk_hi"), sem("qk_lo"), sem("dup_in")
        v_full, vt_ready, turn_full, v_hi, v_lo = sem("v_full"), sem("vt_ready"), sem("turn_full"), sem("v_hi"), sem("v_lo")
        mx_full, mx_free = sem("mx_full"), [sem("mx_free0"), sem("mx_free1")]
        nm_ready, nm_full, nm_t_ready = sem("nm_ready"), sem("nm_full"), sem("nm_t_ready")
        row_in = [sem(f"row_in{q}") for q in range(NT)]
        s_ready, e_ready, ph_ready, pl_ready = sem("s_ready"), sem("e_ready"), sem("ph_ready"), sem("pl_ready")
        acc_step, acc_ready, pv_done = sem("acc_step"), sem("acc_ready"), sem("pv_done")
        fold_full = sem("fold_full")
        ot_ready, rden_ready, o_ready, o_out = sem("ot_ready"), sem("rden_ready"), sem("o_ready"), [sem("o_out0"), sem("o_out1")]
        ob_in = [sem(f"ob_in{t}") for t in range(NT)]
        wo_in, wo_hi, wo_lo = sem("wo_in"), sem("wo_hi"), sem("wo_lo")
        bn2_done, mv2_done, ve2_ready, std2_ready, inv2_ready = (sem("bn2_done"), sem("mv2_done"), sem("ve2_ready"),
                                                                 sem("std2_ready"), sem("inv2_ready"))
        on_ready, tr_ready, aff_ready, onh_ready, onl_ready = (sem("on_ready"), sem("tr_ready"), sem("aff_ready"),
                                                               sem("onh_ready"), sem("onl_ready"))
        po_ready, y_ready = sem("po_ready"), sem("y_ready")
        z_in = [sem(f"z_in{i}") for i in range(4)]
        y_out = [sem(f"y_out{i}") for i in range(4)]

        block = ctx.enter_context(nc.Block())

        @block.sync
        def _(sp):
            with nc.allow_non_contiguous_dma(reason="per-channel parameters"):
                for i, v in enumerate((gamma1, beta1, gamma2, beta2, b_out)):
                    sp.dma_start(par[:, i, :], v.rearrange("(k p) -> p k", p=P)).then_inc(par_in, 16)

            def load_qk_weights(b_h, h):
                sp.wait_ge(qk_lo, h * NT)
                sp.wait_ge(wq_lo, h)
                for i in range(2):
                    col = b_h * DH + i * C
                    sp.dma_start(wq_raw[:, :, i * DH:(i + 1) * DH], w_v[:, :, bass.ds(col, DH)]).then_inc(wq_in, 16)
                    sp.dma_start(b_qk[i * DH:(i + 1) * DH, :],
                                 b_qkv[bass.ds(col, DH)].rearrange("(p o) -> p o", o=1)).then_inc(wq_in, 16)

            def load_v_weights(b_p, pair):
                sp.wait_ge(vt_ready, pair * NT)
                sp.wait_ge(wv_lo, pair)
                col = b_p * P + 2 * C
                sp.dma_start(wv_raw[:, :, :], w_v[:, :, bass.ds(col, P)]).then_inc(wv_in, 16)
                sp.dma_start(b_v[:, :], b_qkv[bass.ds(col, P)].rearrange("(p o) -> p o", o=1)).then_inc(wv_in, 16)

            def duplicate(h, s, t):
                sp.wait_ge(qk_hi, h * NT + t + 1)
                w = slice(t * W, (t + 1) * W)
                sp.dma_start(q_hh[s][DH:P, w].bitcast(F32), q_hh[s][0:DH, w].bitcast(F32)).then_inc(dup_in, 16)
                sp.dma_start(k_h1[s][0:DH, w].bitcast(F32), k_hl[s][0:DH, w].bitcast(F32)).then_inc(dup_in, 16)

            def max_row(h, s, q):
                sp.wait_ge(nm_t_ready, h * NT + q + 1)
                sp.dma_start(q_lm[s][DH:DH + 1, q * W:(q + 1) * W].bitcast(F32).rearrange("o (a b) -> o a b", a=4),
                             nm_t[:, q % 2, :].bitcast(F32)).then_inc(row_in[q], 16)

            def store_heads(b, b_h, h, q):
                sp.wait_ge(o_ready, h * NT + q + 1)
                sp.dma_start(o_v[bass.ds(b, 1), :, q * 4:(q + 1) * 4, bass.ds(b_h * DH, DH)].rearrange("o p t c -> (o p) t c"),
                             o_st[:, q % 2, :, :]).then_inc(o_out[q % 2], 16)

            def beside_last(b, slot, u):
                if u == LOAD_WO:
                    sp.wait_ge(turn_full, slot.h * NT + NT)
                    sp.dma_start(wo_raw, wo_v).then_inc(wo_in, 16)
                if u == LOAD_OB:
                    sp.wait_ge(pv_done, slot.units)
                    for i in range(2):
                        sp.wait_ge(o_out[i], slot.stores)
                    for t in range(NT):
                        sp.dma_start(ob[:, t * 4:(t + 1) * 4, 0:C - DH],
                                     o_v[bass.ds(b, 1), :, t * 4:(t + 1) * 4, 0:C - DH].rearrange("o p t c -> (o p) t c")
                                     ).then_inc(ob_in[t], 16)
                if u == LOAD_Z:
                    sp.wait_ge(wo_lo, b + 1)
                    sp.wait_ge(z_out, b * (16 * NT) + 16 * NT)
                    for c in range(NK):
                        load_z(b, 0, c)

            def load_z(b, t, c):
                sp.dma_start(z_st[:, c, :],
                             z_dram[bass.ds(b, 1), :, c, t * W:(t + 1) * W].rearrange("o p t -> (o p) t")).then_inc(z_in[c], 16)

            def load_x(b, ahead):
                for k in range(NK):
                    sp.dma_start(xb[:, k, :], x_v[bass.ds(b + ahead, 1), :, k, :].rearrange("o p t -> (o p) t")).then_inc(x_in[k], 16)

            load_x(0, 0)

            def beside(b, p, slot, u):
                s, b_h = slot.odd, p * 2 + slot.odd
                if not slot.has_next:
                    beside_last(b, slot, u)
                if u in FOLD and not (slot.first and u == LAG) and (slot.has_next or FOLD[u] < 0):
                    q = FOLD[u]
                    store_heads(b, b_h + (-1 if q < 0 else 0), slot.h + (-1 if q < 0 else 0), q % NT)
                if u == LOAD_WEIGHTS and slot.has_pair:
                    load_qk_weights(b_h + 2, slot.h + 2)
                    if not slot.odd:
                        load_v_weights(p + 1, slot.pair + 1)
                t = ended(QK_PROJ, u)
                if t is not None and slot.has_next:
                    duplicate(slot.h + 1, 1 - s, t)
                if u in NM_TURN:
                    ahead, q = divmod(NM_TURN[u], NT)
                    if not ahead or slot.has_next:
                        max_row(slot.h + ahead, s ^ ahead, q)

            def batch(b, final=False):
                load_qk_weights(0, b * HEADS)
                load_v_weights(0, b * (HEADS // 2))
                for t in range(NT):
                    w = slice(t * W, (t + 1) * W)
                    sp.wait_ge(z_ready, b * NT + t + 1)
                    sp.dma_start(z_dram[bass.ds(b, 1), :, :, w].rearrange("o p k t -> (o p) k t"), xb[:, :, w]).then_inc(z_out, 16)
                for t in range(NT):
                    duplicate(b * HEADS, 0, t)
                load_qk_weights(1, b * HEADS + 1)
                h, units = b * HEADS, opening(b)
                sp.wait_ge(rows_set, b * 4 + 2)
                max_row(h, 0, 0)
                for slot, u in units:
                    beside(b, 0, slot, u)
                with sp.Fori(0, HEADS // 2 - 1) as p:
                    for i, (slot, u) in enumerate(turn(b, p)):
                        beside(b, p if i < 2 * UNITS - OPEN else p + 1, slot, u)
                for slot, u in turn(b, HEADS // 2 - 1, last_pair=True):
                    beside(b, HEADS // 2 - 1, slot, u)
                if not final:
                    sp.wait_ge(pv_done, b * (HEADS * UNITS) + HEADS * UNITS)
                    load_x(b, 1)

                def store_y(t, c):
                    n = t * NK + c
                    sp.wait_ge(y_ready, b * (NT * NK) + n + 1)
                    sp.dma_start(out_v[bass.ds(b, 1), :, c, t * W:(t + 1) * W].rearrange("o p t -> (o p) t"),
                                 z_st[:, c, :]).then_inc(y_out[c], 16)

                for t in range(NT):
                    for c in range(NK):
                        store_y(t, c)
                        if t + 1 < NT:
                            sp.wait_ge(y_out[c], b * (16 * NT) + 16 * (t + 1))
                            load_z(b, t + 1, c)

            with sp.Fori(0, BATCH - 1) as b:
                batch(b)
            batch(BATCH - 1, final=True)
            for c in range(NK):
                sp.wait_ge(y_out[c], BATCH * 16 * NT)

        @block.gpsimd
        def _(pool):
            for tile, value in ((ident, 0.0), (zero, 0.0), (ones, 1.0), (avg_c, 1.0 / C), (avg_g, 1.0 / GROUP)):
                nc.gpsimd.memset(tile[:, :], value).then_inc(const_set, 1)
            pool.wait_ge(const_set, 5)
            nc.gpsimd.affine_select(out=ident[:, :], in_=ident[:, :], compare_op=ALU.not_equal, fill=1.0, base=0,
                                    pattern=[[-1, P]], channel_multiplier=1).then_inc(const_ready, 1)
            groups = avg_g[:, :].rearrange("p (g i) -> p g i", i=GROUP)
            nc.gpsimd.affine_select(out=groups, in_=groups, compare_op=ALU.is_ge, fill=0.0, base=0,
                                    pattern=[[-GROUP, P // GROUP], [0, GROUP]], channel_multiplier=1).then_inc(const_set, 1)
            pool.wait_ge(const_set, 6)
            nc.gpsimd.affine_select(out=groups, in_=groups, compare_op=ALU.is_ge, fill=0.0, base=GROUP - 1,
                                    pattern=[[GROUP, P // GROUP], [0, GROUP]], channel_multiplier=-1).then_inc(const_ready, 1)

            def unit(slot, u):
                q, j = divmod(u, UPB)
                pool.wait_ge(e_ready, slot.units * 2 + (2 * u + 2))
                two = [probs[:, u % 2, i * W:(i + 1) * W] for i in range(2)]
                if j == 0:
                    if q > 1 or not slot.first:
                        pool.wait_ge(fold_full, slot.h * NT + (q - 1))
                    nc.gpsimd.tensor_tensor(acc[:, q % 2, :], two[0], two[1], ALU.add).then_inc(acc_ready, 1)
                else:
                    pool.wait_ge(acc_ready, slot.units + u)
                    nc.gpsimd.tensor_tensor(acc[:, q % 2, :], acc[:, q % 2, :], two[0], ALU.add).then_inc(acc_step, 1)
                    pool.wait_ge(acc_step, slot.h * (UNITS - NT) + (u - q))
                    nc.gpsimd.tensor_tensor(acc[:, q % 2, :], acc[:, q % 2, :], two[1], ALU.add).then_inc(acc_ready, 1)

            def batch(b, final=False):
                for t in range(NT):
                    w = slice(t * W, (t + 1) * W)
                    pool.wait_ge(xn_ready, b * NT + t + 1)
                    nc.gpsimd.tensor_tensor(xb[:, :, w], xb[:, :, w], gb[:, :, w], ALU.add).then_inc(z_ready, 1)
                for s in range(2):
                    if s == 0:
                        pool.wait_ge(z_ready, (b + 1) * NT)
                        pool.wait_ge(xl_ready, (b + 1) * NT)
                    else:
                        pool.wait_ge(z_out, (b + 1) * (16 * NT))
                    zeros, one = (c[DH:P, 0:1].to_broadcast([P - DH, T]) for c in (zero, ones))
                    nc.gpsimd.tensor_tensor(k_h1[s][DH:P, :], one, zeros, ALU.add).then_inc(rows_set, 1)
                    nc.gpsimd.tensor_tensor(q_lm[s][DH:P, :], zeros, zeros, ALU.add).then_inc(rows_set, 1)
                for slot, u in opening(b):
                    unit(slot, u)
                with pool.Fori(0, HEADS // 2 - 1) as p:
                    for slot, u in turn(b, p):
                        unit(slot, u)
                for slot, u in turn(b, HEADS // 2 - 1, last_pair=True):
                    unit(slot, u)

            with pool.Fori(0, BATCH - 1) as b:
                batch(b)
            batch(BATCH - 1, final=True)

        @block.scalar
        def _(act):
            def split_qk(h):
                act.wait_ge(wq_in, h * 64 + 64)
                act.wait_ge(qk_full, h * NT)
                nc.scalar.activation(wq_h[:, :, :], wq_raw[:, :, :], ACT.Copy).then_inc(wq_hi, 1)

            def split_v(pair):
                act.wait_ge(wv_in, pair * 32 + 32)
                act.wait_ge(v_full, pair * NT)
                nc.scalar.activation(wv_h[:, :, :], wv_raw[:, :, :], ACT.Copy).then_inc(wv_hi, 1)

            def qk_halves(h, s, t, free, bank=BANK_PROJ):
                act.wait_ge(pv_done, free)
                act.wait_ge(qk_full, h * NT + (t + 1))
                w = slice(t * W, (t + 1) * W)
                nc.scalar.activation(q_hh[s][0:DH, w], ps[0:DH, bank, :], ACT.Identity, bias=b_qk[0:DH, :])
                nc.scalar.activation(k_hl[s][0:DH, w], ps[DH:P, bank, :], ACT.Identity,
                                     bias=b_qk[DH:P, :]).then_inc(qk_hi, 1)

            def v_rows(pair, t, bank=BANK_PROJ):
                act.wait_ge(v_full, pair * NT + (t + 1))
                nc.scalar.activation(vt[:, t * W:(t + 1) * W], ps[:, bank, :], ACT.Identity,
                                     bias=b_v[:, :]).then_inc(vt_ready, 1)

            def v_halves(h, s, t, free, bank=BANK_PROJ):
                act.wait_ge(turn_full, h * NT + (t + 1))
                act.wait_ge(pv_done, free)
                src = ps[:, bank, :].rearrange("p (t c) -> p t c", c=P)[:, :, s * DH:(s + 1) * DH]
                nc.scalar.activation(v_hl[:, s, t * 4:(t + 1) * 4, 0:DH], src, ACT.Copy).then_inc(v_hi, 1)

            def max_columns(h, q):
                act.wait_ge(nm_full, h * NT + (q + 1))
                act.wait_ge(row_in[(q + 2) % NT], h * 16 if q < 2 else h * 16 + 16)
                nc.scalar.activation(nm_t[:, q % 2, :], ps[0:4, BANK_MISC, 0:P], ACT.Copy).then_inc(nm_t_ready, 1)

            def take_output(slot, q):
                act.wait_ge(pv_done, slot.units + (q + 1) * UPB)
                act.wait_ge(fold_full, slot.h * NT + q)
                nc.scalar.activation(ot[:, :], ps[:, BANK_PV, :], ACT.Copy).then_inc(ot_ready, 1)

            def unit(slot, u):
                s = slot.odd
                if u in FOLD and not (slot.first and u == LAG):
                    take_output(slot, FOLD[u])
                t = ended(QK_PROJ, u)
                if t is not None and slot.has_next:
                    qk_halves(slot.h + 1, 1 - s, t, slot.units)
                t = ended(V_PROJ, u)
                if t is not None and slot.has_pair and slot.odd:
                    v_rows(slot.pair + 1, t)
                if u - 1 in V_TURN[slot.odd] and slot.has_next:
                    v_halves(slot.h + 1, 1 - s, V_TURN[slot.odd][u - 1], slot.units)
                if u - 1 in NM_TURN:
                    ahead, q = divmod(NM_TURN[u - 1], NT)
                    if not ahead or slot.has_next:
                        max_columns(slot.h + ahead, q)
                if u == SPLIT_QK and slot.has_pair:
                    split_qk(slot.h + 2)
                if u == SPLIT_V and slot.has_pair and not slot.odd:
                    split_v(slot.pair + 1)
                act.wait_ge(pl_ready, slot.two_before(u))
                act.wait_ge(acc_ready, slot.two_before(u))
                for i in range(2):
                    act.wait_ge(s_ready, slot.units * 2 + (2 * u + i + 1))
                    e = nc.scalar.activation(probs[:, u % 2, i * W:(i + 1) * W], ps[:, BANK_S[(2 * u + i + 64 * s) % 3], :],
                                             ACT.Exp, scale=SCALE).then_inc(e_ready, 1)
                act.wait_ge(e_ready, slot.units * 2 + (2 * u + 2))
                act.wait_ge(pv_done, slot.two_before(u))
                nc.scalar.activation(ph[:, u % 2, :], probs[:, u % 2, :], ACT.Copy).then_inc(ph_ready, 1)

            def group_std(b, ahead):
                act.wait_ge(gn_dve, b * 4 + (4 * ahead + 3))
                nc.scalar.activation(gs[:, :], gv[:, :], ACT.Sqrt).then_inc(gn_std, 1)

            def output_std(b, t):
                act.wait_ge(ve2_ready, b * NT + t + 1)
                nc.scalar.activation(rs2[:, t * 4:(t + 1) * 4], rs2[:, t * 4:(t + 1) * 4], ACT.Sqrt).then_inc(std2_ready, 1)

            def output_hi(b, t, k):
                n = t * NK + k
                act.wait_ge(tr_ready, b * (NT * NK) + n + 1)
                if n > 1:
                    act.wait_ge(onl_ready, b * (NT * NK) + n - 1)
                nc.scalar.activation(on_st[n % 2], ps[:, BANK_TURN, :], ACT.Identity, scale=par[:, 2, k:k + 1],
                                     bias=par[:, 3, k:k + 1]).then_inc(aff_ready, 1)
                act.wait_ge(aff_ready, b * (NT * NK) + n + 1)
                nc.scalar.activation(xh[:, k, t * W:(t + 1) * W], on_st[n % 2], ACT.Copy).then_inc(onh_ready, 1)

            def beside_last(b, u):
                if u == SPLIT_WO:
                    act.wait_ge(wo_in, b * 16 + 16)
                    nc.scalar.activation(wo_h, wo_raw, ACT.Copy).then_inc(wo_hi, 1)
                if u == OUT_NORM:
                    for t in range(OUT_EARLY):
                        output_std(b, t)
                if u - 1 in OUT_TURN:
                    output_hi(b, *OUT_TURN[u - 1])

            act.wait_ge(par_in, 80)
            group_std(0, 0)
            def batch(b, final=False):
                for i in range(NT + 2):
                    t = i
                    if t < NT:
                        act.wait_ge(dev_ready, b * NT + t + 1)
                        if t > 1:
                            act.wait_ge(var_ready, b * NT + (t - 1))
                        nc.scalar.activation(sq[t % 2], gb[:, :, t * W:(t + 1) * W], ACT.Square).then_inc(sq_ready, 1)
                    t = i - 1
                    if 0 <= t < NT:
                        r = rstd[:, 4 * t:4 * t + 4]
                        act.wait_ge(veps_ready, b * NT + t + 1)
                        nc.scalar.activation(r, r, ACT.Sqrt, scale=1.0 / C ** 2).then_inc(std_ready, 1)
                    t = i - 2
                    if 0 <= t:
                        act.wait_ge(norm_ready, b * NT + t + 1)
                        if t == 0:
                            act.wait_ge(po_ready, b * (NT * NK))
                        for k in range(NK):
                            w = gb[:, k, t * W:(t + 1) * W]
                            xn = nc.scalar.activation(w, w, ACT.Identity, scale=par[:, 0, k:k + 1], bias=par[:, 1, k:k + 1])
                        xn.then_inc(xn_ready, 1)
                        act.wait_ge(xn_ready, b * NT + t + 1)
                        nc.scalar.activation(xh[:, :, t * W:(t + 1) * W], gb[:, :, t * W:(t + 1) * W], ACT.Copy).then_inc(xh_ready, 1)
                    if i == 2:
                        split_qk(b * HEADS)
                    if i == 3:
                        split_v(b * (HEADS // 2))
                for t in range(NT):
                    act.wait_ge(z_ready, b * NT + t + 1)
                    act.wait_ge(xl_ready, b * NT + t + 1)
                    qk_halves(b * HEADS, 0, t, b * (HEADS * UNITS), bank=t)
                for t in range(NT):
                    v_rows(b * (HEADS // 2), t, bank=4 + t)
                for t in range(NT):
                    v_halves(b * HEADS, 0, t, b * (HEADS * UNITS), bank=t)
                act.wait_ge(rows_set, (b + 1) * 4)
                max_columns(b * HEADS, 0)
                split_qk(b * HEADS + 1)
                for slot, u in opening(b):
                    unit(slot, u)
                with act.Fori(0, HEADS // 2 - 1) as p:
                    for slot, u in turn(b, p):
                        unit(slot, u)
                for slot, u in turn(b, HEADS // 2 - 1, last_pair=True):
                    if not slot.has_next:
                        beside_last(b, u)
                    unit(slot, u)
                take_output(Slot(b + 1, 0, 0), -1)
                output_std(b, 2)
                for n in range(2 * NK, NT * NK):
                    if n == 2 * NK + 2:
                        output_std(b, 3)
                    output_hi(b, *divmod(n, NK))
                if not final:
                    group_std(b, 1)

            with act.Fori(0, BATCH - 1) as b:
                batch(b)
            batch(BATCH - 1, final=True)

        @block.vector
        def _(dve):
            def split_qk(h):
                dve.wait_ge(wq_hi, h + 1)
                nc.vector.tensor_tensor(wq_l[:, :, :], wq_raw[:, :, :], wq_h[:, :, :], ALU.subtract).then_inc(wq_lo, 1)

            def split_v(pair):
                dve.wait_ge(wv_hi, pair + 1)
                nc.vector.tensor_tensor(wv_l[:, :, :], wv_raw[:, :, :], wv_h[:, :, :], ALU.subtract).then_inc(wv_lo, 1)

            def qk_remainders(h, s, t, bank=BANK_PROJ):
                dve.wait_ge(qk_hi, h * NT + t + 1)
                w = slice(t * W, (t + 1) * W)
                nc.vector.scalar_tensor_tensor(out=q_lm[s][0:DH, w], in0=ps[0:DH, bank, :], scalar=b_qk[0:DH, :],
                                               in1=q_hh[s][0:DH, w], op0=ALU.add, op1=ALU.subtract)
                nc.vector.scalar_tensor_tensor(out=k_hl[s][DH:P, w], in0=ps[DH:P, bank, :], scalar=b_qk[DH:P, :],
                                               in1=k_hl[s][0:DH, w], op0=ALU.add, op1=ALU.subtract).then_inc(qk_lo, 1)

            def v_remainders(h, s, t, bank=BANK_PROJ):
                dve.wait_ge(v_hi, h * NT + t + 1)
                src = ps[:, bank, :].rearrange("p (t c) -> p t c", c=P)[:, :, s * DH:(s + 1) * DH]
                nc.vector.tensor_tensor(v_hl[:, s, t * 4:(t + 1) * 4, DH:P], src, v_hl[:, s, t * 4:(t + 1) * 4, 0:DH],
                                        ALU.subtract).then_inc(v_lo, 1)

            def reduce_max(h, q, step, base, half, n):
                dve.wait_ge(mx_full, base + (n + 1))
                i, kc = divmod(step, NT)
                nc.vector.tensor_reduce(nm4[:, q % 2, i, kc:kc + 1], ps[:, BANK_MX[n % 2], :], op=ALU.max, axis=AX.X,
                                        negate=True).then_inc(mx_free[n % 2], 1)
                if step == 4 * NT - 1:
                    for parity in range(2):
                        dve.wait_ge(mx_free[parity], half + (n + 2 - parity) // 2)
                    nc.vector.tensor_reduce(nm[:, q % 2, :], nm4[:, q % 2, :, :], op=ALU.min, axis=AX.X).then_inc(nm_ready, 1)

            def take_fold(h, q, stores, direct=False):
                dve.wait_ge(fold_full, h * NT + (q + 1))
                src = ps[:, BANK_MISC, 0:4 * (DH + 1)].rearrange("p (t c) -> p t c", c=DH + 1)
                nc.vector.reciprocal(rden[:, :], src[:, :, DH]).then_inc(rden_ready, 1)
                dve.wait_ge(rden_ready, h * NT + (q + 1))
                if not direct:
                    dve.wait_ge(o_out[q % 2], stores + 16 * (q // 2))
                dest = ob[:, q * 4:(q + 1) * 4, C - DH:C] if direct else o_st[:, q % 2, :, :]
                nc.vector.tensor_tensor(dest, src[:, :, 0:DH],
                                        rden[:, :].rearrange("p (t o) -> p t o", o=1).to_broadcast([P, 4, DH]),
                                        ALU.mult).then_inc(o_ready, 1)

            def output_stats(b, t):
                dve.wait_ge(ob_in[t], b * 16 + 16)
                dve.wait_ge(o_ready, b * (HEADS * NT) + ((HEADS - 1) * NT + t + 1))
                for i in range(4 * t, 4 * t + 4):
                    nc.vector.bn_stats(bn2[:, i, :], ob[:, i, :]).then_inc(bn2_done, 1)
                dve.wait_ge(bn2_done, b * KB + 4 * t + 4)
                nc.vector.memset(carrier[:, :], 0.0)
                for i in range(4 * t, 4 * t + 4):
                    nc.vector.bn_aggr(mv2[:, i, :], bn2[:, i, :]).then_inc(mv2_done, 1)
                dve.wait_ge(mv2_done, b * KB + 4 * t + 4)
                nc.vector.tensor_scalar(rs2[:, 4 * t:4 * t + 4], mv2[:, 4 * t:4 * t + 4, 1], EPS, None,
                                        ALU.add).then_inc(ve2_ready, 1)

            def output_norm(b, t):
                r = rs2[:, 4 * t:4 * t + 4]
                dve.wait_ge(std2_ready, b * NT + t + 1)
                nc.vector.reciprocal(r, r).then_inc(inv2_ready, 1)
                dve.wait_ge(inv2_ready, b * NT + t + 1)
                for i in range(4 * t, 4 * t + 4):
                    on = nc.vector.tensor_scalar(ob[:, i, :], ob[:, i, :], mv2[:, i, 0:1], rs2[:, i:i + 1],
                                                 ALU.subtract, ALU.mult)
                on.then_inc(on_ready, 1)

            def output_lo(b, t, k):
                n = t * NK + k
                dve.wait_ge(onh_ready, b * (NT * NK) + n + 1)
                nc.vector.tensor_tensor(xl[:, k, t * W:(t + 1) * W], on_st[n % 2], xh[:, k, t * W:(t + 1) * W],
                                        ALU.subtract).then_inc(onl_ready, 1)

            def residual(b, t, c):
                n = t * NK + c
                dve.wait_ge(po_ready, b * (NT * NK) + n + 1)
                dve.wait_ge(z_in[c], b * (16 * NT) + 16 * (t + 1))
                nc.vector.scalar_tensor_tensor(out=z_st[:, c, :], in0=ps[:, BANK_OUT[n % 2], :], scalar=par[:, 4, c:c + 1],
                                               in1=z_st[:, c, :], op0=ALU.add, op1=ALU.add).then_inc(y_ready, 1)

            def beside_last(b, u):
                if u == SPLIT_WO:
                    dve.wait_ge(wo_hi, b + 1)
                    nc.vector.tensor_tensor(wo_l, wo_raw, wo_h, ALU.subtract).then_inc(wo_lo, 1)
                if u in OUT_STATS:
                    output_stats(b, OUT_STATS[u])
                if u == OUT_NORM:
                    for t in range(OUT_EARLY):
                        output_norm(b, t)
                if u - 1 in OUT_TURN:
                    output_lo(b, *OUT_TURN[u - 1])

            def channel_stats(b, ahead, k):
                dve.wait_ge(x_in[k], b * 16 + (ahead * 16 + 16))
                for t in range(NT):
                    nc.vector.bn_stats(bn[:, k, t, :], xb[:, k, t * W:(t + 1) * W]).then_inc(bn_done, 1)

            def channel_moments(b, ahead):
                dve.wait_ge(bn_done, b * (NK * NT) + (ahead + 1) * (NK * NT))
                nc.vector.memset(carrier[:, :], 0.0)
                for k in range(NK):
                    nc.vector.bn_aggr(mv[:, k, :], bn[:, k, :, :]).then_inc(gn_in if k == NK - 1 else bn_agg, 1)

            def group_moments(b, ahead):
                dve.wait_ge(gn_sum, b * 2 + (ahead * 2 + 1))
                nc.vector.tensor_copy(gm[:, :], ps[:, BANK_MISC, 0:NK]).then_inc(gn_dve, 1)
                dve.wait_ge(gn_dve, b * 4 + (ahead * 4 + 1))
                nc.vector.tensor_tensor(gv[:, :], mv[:, :, 0], gm[:, :], ALU.subtract).then_inc(bn_agg, 1)
                dve.wait_ge(bn_agg, b * (NK + 1) + (ahead * (NK + 1) + NK))
                nc.vector.tensor_tensor(gv[:, :], gv[:, :], gv[:, :], ALU.mult).then_inc(bn_agg, 1)
                dve.wait_ge(bn_agg, b * (NK + 1) + (ahead * (NK + 1) + NK + 1))
                nc.vector.tensor_tensor(gs[:, :], gv[:, :], mv[:, :, 1], ALU.add).then_inc(gn_dve, 1)

            def group_variance(b, ahead):
                dve.wait_ge(gn_sum, b * 2 + (ahead * 2 + 2))
                nc.vector.tensor_scalar(gv[:, :], ps[:, BANK_MISC, 0:NK], EPS, None, ALU.add).then_inc(gn_dve, 1)

            def group_scale(b, ahead):
                dve.wait_ge(gn_std, b + (ahead + 1))
                nc.vector.reciprocal(gs[:, :], gs[:, :]).then_inc(gn_dve, 1)

            def group_norm(b, ahead, k):
                dve.wait_ge(gn_dve, b * 4 + (ahead * 4 + 4))
                nc.vector.tensor_scalar(gb[:, k, :], xb[:, k, :], gm[:, k:k + 1], gs[:, k:k + 1], ALU.subtract,
                                        ALU.mult).then_inc(g_ready, 1)

            def unit(slot, u, b=None):
                s = slot.odd
                if u - 1 in FOLD and not (slot.first and u - 1 == LAG):
                    q = FOLD[u - 1]
                    if q < 0:
                        take_fold(slot.h - 1, NT - 1, slot.stores - 16 * NT // 2)
                    else:
                        take_fold(slot.h, q, slot.stores, direct=not slot.has_next)
                t = ended(QK_PROJ, u)
                if t is not None and slot.has_next:
                    qk_remainders(slot.h + 1, 1 - s, t)
                if u - 1 in V_TURN[slot.odd] and slot.has_next:
                    v_remainders(slot.h + 1, 1 - s, V_TURN[slot.odd][u - 1])
                if u == SPLIT_QK and slot.has_pair:
                    split_qk(slot.h + 2)
                if u == SPLIT_V and slot.has_pair and not slot.odd:
                    split_v(slot.pair + 1)
                for i, (ahead, q, step) in enumerate(max_steps(slot, u)):
                    reduce_max(slot.h + ahead, q, step, slot.mx, slot.mx_half, 2 * u + i)
                if not slot.has_next:
                    beside_last(b, u)
                dve.wait_ge(ph_ready, slot.units + (u + 1))
                dve.wait_ge(pv_done, slot.two_before(u))
                nc.vector.tensor_tensor(pl[:, u % 2, :], probs[:, u % 2, :], ph[:, u % 2, :],
                                        ALU.subtract).then_inc(pl_ready, 1)

            dve.wait_ge(par_in, 80)
            dve.wait_ge(const_ready, 1)
            nc.vector.tensor_tensor(fold[:, :], ident[:, 0:DH], ident[:, DH:P], ALU.add).then_inc(fold_ready, 1)
            for k in range(NK):
                channel_stats(0, 0, k)
            for step in (channel_moments, group_moments, group_variance, group_scale):
                step(0, 0)
            for k in range(NK):
                group_norm(0, 0, k)

            def batch(b, final=False):
                dve.wait_ge(g_ready, (b + 1) * NK)
                for i in range(NT + 3):
                    t = i
                    if t < NT:
                        dve.wait_ge(mean_ready, b * NT + t + 1)
                        w = gb[:, :, t * W:(t + 1) * W]
                        mean = ps[:, t:t + 1, :].to_broadcast([P, NK, W])
                        nc.vector.tensor_tensor(w, w, mean, ALU.subtract).then_inc(dev_ready, 1)
                    t = i - 1
                    if 0 <= t < NT:
                        r = rstd[:, 4 * t:4 * t + 4]
                        dve.wait_ge(var_ready, b * NT + t + 1)
                        nc.vector.tensor_scalar(r, ps[:, 6 + t % 2, 0:4], EPS, None, ALU.add).then_inc(veps_ready, 1)
                        dve.wait_ge(std_ready, b * NT + t + 1)
                        nc.vector.reciprocal(r, r).then_inc(inv_ready, 1)
                        dve.wait_ge(inv_ready, b * NT + t + 1)
                        nc.vector.tensor_tensor(diag[t].rearrange("p (i c) -> p i c", c=P),
                                                ident[:, :].rearrange("p (o c) -> p o c", o=1).to_broadcast([P, 4, P]),
                                                r.rearrange("p (i o) -> p i o", o=1).to_broadcast([P, 4, P]),
                                                ALU.mult).then_inc(diag_ready, 1)
                    t = i - 2
                    if 0 <= t < NT:
                        dve.wait_ge(spread_ready, b * NT + t + 1)
                        w = gb[:, :, t * W:(t + 1) * W]
                        nc.vector.tensor_tensor(w, w, ps[:, 6 + t % 2:7 + t % 2, :].to_broadcast([P, NK, W]),
                                                ALU.mult).then_inc(norm_ready, 1)
                    t = i - 3
                    if 0 <= t:
                        w = slice(t * W, (t + 1) * W)
                        dve.wait_ge(xh_ready, b * NT + t + 1)
                        nc.vector.tensor_tensor(xl[:, :, w], gb[:, :, w], xh[:, :, w], ALU.subtract).then_inc(xl_ready, 1)
                    if i == 2:
                        split_qk(b * HEADS)
                    if i == 3:
                        split_v(b * (HEADS // 2))
                for t in range(NT):
                    dve.wait_ge(z_ready, b * NT + t + 1)
                    qk_remainders(b * HEADS, 0, t, bank=t)
                for n in range(PRO_MX):
                    q, step = divmod(n, 16)
                    reduce_max(b * HEADS, q, step, b * BATCH_MX, b * (BATCH_MX // 2), n)
                    if n - 2 in PRO_TURN:
                        v_remainders(b * HEADS, 0, PRO_TURN[n - 2], bank=PRO_TURN[n - 2])
                split_qk(b * HEADS + 1)
                for slot, u in opening(b):
                    unit(slot, u)
                with dve.Fori(0, HEADS // 2 - 1) as p:
                    for slot, u in turn(b, p):
                        unit(slot, u)
                for slot, u in turn(b, HEADS // 2 - 1, last_pair=True):
                    unit(slot, u, b)
                output_norm(b, 2)
                take_fold(b * HEADS + (HEADS - 1), NT - 1, 0, direct=True)
                output_stats(b, 3)
                for c in range(NK):
                    output_lo(b, 2, c)
                    if c == 1:
                        output_norm(b, 3)
                    residual(b, 0, c)
                for c in range(NK):
                    output_lo(b, 3, c)
                    residual(b, 1, c)
                    if not final:
                        channel_stats(b, 1, c)
                steps = [channel_moments, group_moments, group_variance, group_scale]
                for c in range(NK):
                    if not final:
                        steps[c](b, 1)
                    residual(b, 2, c)
                for c in range(NK):
                    if not final:
                        group_norm(b, 1, c)
                    residual(b, 3, c)

            with dve.Fori(0, BATCH - 1) as b:
                batch(b)
            batch(BATCH - 1, final=True)

        @block.tensor
        def _(pe):
            def project(w_h, w_l, t, part, parts, full, bank=BANK_PROJ):
                w = slice(t * W, (t + 1) * W)
                terms = [(a, k, x) for k in range(NK) for a, x in ((w_h, xh), (w_l, xh), (w_h, xl))]
                n = len(terms) // parts
                for i, (a, k, x) in enumerate(terms[part * n:(part + 1) * n], part * n):
                    last = nc.tensor.matmul(ps[:, bank, :], a[:, k, :], x[:, k, w], start=(i == 0),
                                            stop=(i == len(terms) - 1))
                if part == parts - 1:
                    last.then_inc(full, 1)

            def turn_v(h, pair, t, bank=BANK_PROJ):
                pe.wait_ge(vt_ready, pair * NT + (t + 1))
                for i in range(4):
                    last = nc.tensor.transpose(ps[:, bank, i * P:(i + 1) * P],
                                               vt[:, t * W + i * P:t * W + (i + 1) * P], ident[:, :])
                last.then_inc(turn_full, 1)

            def scores_for_max(h, s, q, step, half, n):
                i, kc = divmod(step, NT)
                if step == 0 and q == 0:
                    pe.wait_ge(dup_in, h * (32 * NT) + 32 * NT)
                    pe.wait_ge(qk_lo, h * NT + NT)
                pe.wait_ge(mx_free[n % 2], half + n // 2)
                qs = q * W + i * P
                nc.tensor.matmul(ps[:, BANK_MX[n % 2], :], q_hh[s][:, qs:qs + P], k_hl[s][:, kc * W:(kc + 1) * W],
                                 start=True, stop=True).then_inc(mx_full, 1)

            def turn_max(h, q):
                pe.wait_ge(nm_ready, h * NT + (q + 1))
                nc.tensor.matmul(ps[0:4, BANK_MISC, 0:P], nm[:, q % 2, :], ident[:, :], start=True, stop=True).then_inc(nm_full, 1)

            def fold_output(slot, q):
                pe.wait_ge(ot_ready, slot.h * NT + (q + 1))
                pe.wait_ge(acc_ready, slot.units + (q + 1) * UPB)
                for i in range(4):
                    o, w = i * (DH + 1), slice(i * P, (i + 1) * P)
                    nc.tensor.matmul(ps[:, BANK_MISC, o:o + DH], ot[:, w], fold[:, :], start=True, stop=True)
                    last = nc.tensor.matmul(ps[:, BANK_MISC, o + DH:o + DH + 1], acc[:, q % 2, w], ones[:, :],
                                            start=True, stop=True)
                last.then_inc(fold_full, 1)

            def probs_times_v(slot, u):
                q, j = divmod(u, UPB)
                s = slot.odd if u >= 0 else 1 - slot.odd
                pe.wait_ge(pl_ready, slot.units + (u + 1))
                if j == 0:
                    if u == 0:
                        pe.wait_ge(v_lo, slot.h * NT + NT)
                    if u or not slot.first:
                        pe.wait_ge(ot_ready, slot.h * NT + q)
                for i in range(2):
                    v = v_hl[:, s, 2 * j + i, :]
                    nc.tensor.matmul(ps[:, BANK_PV, :], v, ph[:, u % 2, i * W:(i + 1) * W], start=(j == 0 and i == 0), stop=False)
                    last = nc.tensor.matmul(ps[:, BANK_PV, :], v, pl[:, u % 2, i * W:(i + 1) * W], start=False,
                                            stop=(j == UPB - 1 and i == 1))
                last.then_inc(pv_done, 1)

            def scores(slot, u):
                q, j = divmod(u, UPB)
                s = slot.odd
                if j == 0:
                    pe.wait_ge(row_in[q], slot.h * 16 + 16)
                w = slice(q * W, (q + 1) * W)
                for i in range(2):
                    n = 2 * u + i
                    if n > 2 or not slot.first:
                        back = 1 if n < 2 and not s else 2
                        pe.wait_ge(e_ready, slot.units * 2 + (n - back))
                    k = slice((2 * j + i) * P, (2 * j + i + 1) * P)
                    bank = BANK_S[(n + 64 * s) % 3]
                    nc.tensor.matmul(ps[:, bank, :], k_hl[s][:, k], q_hh[s][:, w], start=True, stop=False)
                    nc.tensor.matmul(ps[:, bank, :], k_h1[s][:, k], q_lm[s][:, w], start=False, stop=True).then_inc(s_ready, 1)

            def unit(slot, u):
                s = slot.odd
                scores(slot, u)
                if u >= LAG or not slot.first:
                    probs_times_v(slot, u - LAG)
                for i, (ahead, q, step) in enumerate(max_steps(slot, u)):
                    scores_for_max(slot.h + ahead, s ^ ahead, q, step, slot.mx_half, 2 * u + i)
                if u in QK_PROJ and slot.has_next:
                    t, part, parts = QK_PROJ[u]
                    if u == 0:
                        pe.wait_ge(v_lo, slot.h * NT + NT)
                        pe.wait_ge(wq_lo, slot.h + 2)
                    elif part == 0:
                        pe.wait_ge(qk_lo, slot.h * NT + (NT + t))
                    project(wq_h, wq_l, t, part, parts, qk_full)
                if u in V_PROJ and slot.odd and slot.has_pair:
                    t, part, parts = V_PROJ[u]
                    if part == 0:
                        if t == 0:
                            pe.wait_ge(qk_lo, slot.h * NT + 2 * NT)
                            pe.wait_ge(wv_lo, slot.pair + 2)
                        else:
                            pe.wait_ge(vt_ready, slot.pair * NT + (NT + t))
                    project(wv_h, wv_l, t, part, parts, v_full)
                if u in V_TURN[slot.odd] and slot.has_next:
                    t = V_TURN[slot.odd][u]
                    if t:
                        pe.wait_ge(v_lo, slot.h * NT + (NT + t))
                    elif not slot.odd:
                        pe.wait_ge(qk_lo, slot.h * NT + 2 * NT)
                    else:
                        pe.wait_ge(vt_ready, slot.pair * NT + 2 * NT)
                    turn_v(slot.h + 1, slot.pair + slot.odd, t)
                if u in NM_TURN:
                    ahead, q = divmod(NM_TURN[u], NT)
                    if not ahead or slot.has_next:
                        if u > AHEAD or not slot.first:
                            pe.wait_ge(o_ready, slot.h * NT + q_folded(u))
                        turn_max(slot.h + ahead, q)
                if u in FOLD and not (slot.first and u == LAG):
                    q = FOLD[u]
                    pe.wait_ge(nm_t_ready, slot.h * NT + (q + 2))
                    fold_output(slot, q)

            def q_folded(u):
                return sum(1 for v, q in FOLD.items() if v < u and q >= 0)

            def turn_outputs(b, t, k):
                n = t * NK + k
                if k == 0:
                    pe.wait_ge(on_ready, b * NT + t + 1)
                if n:
                    pe.wait_ge(aff_ready, b * (NT * NK) + n)
                for i in range(4):
                    last = nc.tensor.transpose(ps[:, BANK_TURN, i * P:(i + 1) * P], ob[:, 4 * t + i, k * P:(k + 1) * P], ident[:, :])
                last.then_inc(tr_ready, 1)

            def project_out(b, t, c):
                n = t * NK + c
                if n == 0:
                    pe.wait_ge(wo_lo, b + 1)
                if n < 2:
                    pe.wait_ge(mx_free[n], b * (BATCH_MX // 2) + BATCH_MX // 2)
                else:
                    pe.wait_ge(y_ready, b * (NT * NK) + n - 1)
                if c == 0:
                    pe.wait_ge(onl_ready, b * (NT * NK) + (t + 1) * NK)
                w, cs = slice(t * W, (t + 1) * W), slice(c * P, (c + 1) * P)
                for k in range(NK):
                    nc.tensor.matmul(ps[:, BANK_OUT[n % 2], :], wo_h[:, k, cs], xh[:, k, w], start=(k == 0), stop=False)
                    nc.tensor.matmul(ps[:, BANK_OUT[n % 2], :], wo_l[:, k, cs], xh[:, k, w], start=False, stop=False)
                    last = nc.tensor.matmul(ps[:, BANK_OUT[n % 2], :], wo_h[:, k, cs], xl[:, k, w], start=False, stop=(k == NK - 1))
                last.then_inc(po_ready, 1)

            def group_sums(b, ahead, i):
                if i == 0:
                    pe.wait_ge(o_ready, (b * HEADS + ahead * HEADS) * NT)
                    pe.wait_ge(gn_in, b + (ahead + 1))
                    pe.wait_ge(bn_agg, b * (NK + 1) + (ahead * (NK + 1) + NK - 1))
                else:
                    pe.wait_ge(gn_dve, b * 4 + (ahead * 4 + 2))
                nc.tensor.matmul(ps[:, BANK_MISC, 0:NK], avg_g[:, :], (mv[:, :, 0], gs[:, :])[i], start=True, stop=True).then_inc(gn_sum, 1)

            def beside_last(b, u):
                if u in OUT_TURN:
                    turn_outputs(b, *OUT_TURN[u])

            pe.wait_ge(const_ready, 2)
            pe.wait_ge(fold_ready, 1)
            for i in range(2):
                group_sums(0, 0, i)

            def batch(b, final=False):
                pe.wait_ge(g_ready, b * NK + NK)

                def mean(t):
                    for k in range(NK):
                        last = nc.tensor.matmul(ps[:, t, :], avg_c[:, :], gb[:, k, t * W:(t + 1) * W], start=(k == 0), stop=(k == NK - 1))
                    last.then_inc(mean_ready, 1)

                for t in range(NT - 1):
                    mean(t)
                for i in range(NT + 1):
                    t = i
                    if t < NT:
                        pe.wait_ge(sq_ready, b * NT + t + 1)
                        if t > 1:
                            pe.wait_ge(norm_ready, b * NT + t - 1)
                        for j in range(4):
                            for k in range(NK):
                                last = nc.tensor.matmul(ps[:, 6 + t % 2, j:j + 1], sq[t % 2][:, k, j * P:(j + 1) * P], avg_c[:, 0:1],
                                                        start=(k == 0), stop=(k == NK - 1))
                        last.then_inc(var_ready, 1)
                    if t == 0:
                        mean(NT - 1)
                    t = i - 1
                    if 0 <= t:
                        pe.wait_ge(diag_ready, b * NT + t + 1)
                        nc.tensor.matmul(ps[:, 6 + t % 2, :], avg_c[:, :], diag[t], start=True, stop=True).then_inc(spread_ready, 1)
                pe.wait_ge(wq_lo, b * HEADS + 1)
                for t, v in ((0, 0), (1, 1), (2, None), (3, 2), (None, 3)):
                    if t is not None:
                        pe.wait_ge(xl_ready, b * NT + t + 1)
                        project(wq_h, wq_l, t, 0, 1, qk_full, bank=t)
                    if v == 0:
                        pe.wait_ge(wv_lo, b * (HEADS // 2) + 1)
                    if v is not None:
                        project(wv_h, wv_l, v, 0, 1, v_full, bank=4 + v)
                pe.wait_ge(vt_ready, b * (HEADS // 2 * NT) + 2)
                for n in range(PRO_MX):
                    if n in PRO_TURN:
                        turn_v(b * HEADS, b * (HEADS // 2), PRO_TURN[n], bank=PRO_TURN[n])
                    q, step = divmod(n, 16)
                    scores_for_max(b * HEADS, 0, q, step, b * (BATCH_MX // 2), n)
                    if n == 15:
                        turn_max(b * HEADS, 0)
                pe.wait_ge(rows_set, (b + 1) * 4)
                pe.wait_ge(v_lo, b * (HEADS * NT) + NT)
                for slot, u in opening(b):
                    unit(slot, u)
                with pe.Fori(0, HEADS // 2 - 1) as p:
                    for slot, u in turn(b, p):
                        unit(slot, u)
                for slot, u in turn(b, HEADS // 2 - 1, last_pair=True):
                    unit(slot, u)
                    if not slot.has_next:
                        beside_last(b, u)
                after = Slot(b + 1, 0, 0)
                for u in range(-LAG, 0):
                    probs_times_v(after, u)
                beside_out = {divmod(1 + n, NK): divmod(OUT_EARLY * NK + n, NK) for n in range((NT - OUT_EARLY) * NK)}
                for t in range(NT):
                    for c in range(NK):
                        if (t, c) in beside_out:
                            turn_outputs(b, *beside_out[t, c])
                        if not final and (t, c) == (2, 2):
                            group_sums(b, 1, 0)
                        if not final and (t, c) == (2, 3):
                            group_sums(b, 1, 1)
                        project_out(b, t, c)
                        if (t, c) == (0, 0):
                            fold_output(after, -1)

            with pe.Fori(0, BATCH - 1) as b:
                batch(b)
            batch(BATCH - 1, final=True)


_INS = ["x", "L0_conv_w_qkv", "L0_conv_b_qkv", "L0_conv_w_out", "L0_conv_b_out", "L0_conv_gamma1", "L0_conv_beta1",
        "L0_conv_gamma2", "L0_conv_beta2"]


def kernel(**inputs):
    import numpy as _np
    import concourse.bacc as _bacc
    from concourse import mybir as _mybir
    from concourse.bass_utils import run_bass_kernel_spmd as _run

    nc = _bacc.Bacc("TRN2", target_bir_lowering=False, num_devices=1)
    arrays, args = {}, []
    for name in _INS:
        a = _np.ascontiguousarray(inputs[name])
        arrays[f"in_{name}_dram"] = a
        args.append(nc.dram_tensor(f"in_{name}_dram", a.shape, _mybir.dt.from_np(a.dtype), kind="ExternalInput").ap())
    args.append(nc.dram_tensor("out_0_dram", (4, 512, 64, 32), _mybir.dt.float32, kind="ExternalOutput").ap())
    program(nc, *args)
    r = _run(nc, [arrays], core_ids=[0])
    return r.results[0]["out_0_dram"]
```

```python
import concourse.bass as bass
from concourse import mybir
from contextlib import ExitStack

F32 = mybir.dt.float32
F32R = mybir.dt.float32r
ALU = mybir.AluOpType
ACT = mybir.ActivationFunctionType
AX = mybir.AxisListType

P = 128
BATCH, C, T = 4, 512, 2048
HEADS = 8
DH = C // HEADS
SCALE = float(DH) ** -0.5
EPS = 1e-5
GROUP = C // 32
NK = C // P
W = 512
NT = T // W
KB = T // P
UPB = KB // 2
UNITS = NT * UPB
LAG = 2

BANK_S = [0, 1, 2]
BANK_PROJ = 3
BANK_MX = [4, 5]
BANK_PV = 6
BANK_MISC = 7

AHEAD = UPB // 2
QK_PROJ = {4 * t + i: (t, i, 3) for t in range(NT) for i in range(3)}
V_PROJ = [{24 + 2 * t + i: (t, i, 2) for t in range(NT // 2) for i in range(2)},
          {16 + 2 * t + i: (NT // 2 + t, i, 2) for t in range(NT // 2) for i in range(2)}]
V_TURN = [{16 + 2 * t: t for t in range(NT)},
          {24 + 2 * t: t for t in range(NT)}]
LOAD_WEIGHTS, SPLIT_QK, SPLIT_V = 16, 21, 23
NM_TURN = {UPB * n + AHEAD: n + 1 for n in range(NT)}
FOLD = {UPB * n + LAG: n - 1 for n in range(NT)}
LOAD_WO, LOAD_OB, LOAD_Z = 1, 5, 14
SPLIT_WO = {8 + k: k for k in range(NK)}
OUT_STATS = {UPB * t + LAG + 10 + i: (t, i) for t in range(NT - 1) for i in range(2)}
OUT_STD = 21
OUT_EARLY = 2
OUT_NORM = {OUT_STD + NK * t: t for t in range(OUT_EARLY)}
OUT_TURN = {OUT_STD + 1 + n: divmod(n, NK) for n in range(OUT_EARLY * NK)}
BANK_TURN = BANK_PROJ
BANK_OUT = BANK_MX
BANK_VAR = [6, 7]
OPEN = 4


def max_steps(slot, u):
    n, s = divmod(2 * (u + AHEAD), 4 * NT)
    return [(*divmod(n + 1, NT), s + i) for i in range(2)] if n + 1 < NT or slot.has_next else []


def ended(plan, u):
    t, part, parts = plan.get(u - 1, (0, 0, 2))
    return t if part == parts - 1 else None


PRO_MX = 24
PRO_TURN = {1 + 3 * t: t for t in range(NT)}
SLOT_MX = 4 * KB
BATCH_MX = SLOT_MX * HEADS


class Slot:

    def __init__(self, b, p, odd, last_pair=False, first=False):
        self.odd, self.first = odd, first
        self.has_next, self.has_pair = not (last_pair and odd), not last_pair
        self.h = b * HEADS + p * 2 + odd
        self.pair = b * (HEADS // 2) + p
        self.stores = (b * (HEADS - 1) + p * 2 + odd) * (16 * NT // 2)
        self.units = self.h * UNITS
        self.mx = b * BATCH_MX + p * (2 * SLOT_MX) + (PRO_MX + odd * SLOT_MX)
        self.mx_half = b * (BATCH_MX // 2) + p * SLOT_MX + (PRO_MX + odd * SLOT_MX) // 2

    def two_before(self, u):
        return self.units + (u - 1 if u > 1 or not self.first else 0)


def opening(b):
    return [(Slot(b, 0, 0, first=True), u) for u in range(OPEN)]


def turn(b, p, last_pair=False):
    even, odd = Slot(b, p, 0, last_pair, first=True), Slot(b, p, 1, last_pair)
    units = [(even, u) for u in range(OPEN, UNITS)] + [(odd, u) for u in range(UNITS)]
    return units + ([] if last_pair else [(Slot(b, p + 1, 0), u) for u in range(OPEN)])


def program(nc, x, w_qkv, b_qkv, w_out, b_out, gamma1, beta1, gamma2, beta2, out):
    x_v = x.rearrange("b (k p) f t -> b p k (f t)", p=P)
    out_v = out.rearrange("b (k p) f t -> b p k (f t)", p=P)
    w_v = w_qkv.rearrange("(k p) n -> p k n", p=P)
    wo_v = w_out.rearrange("(k p) n -> p k n", p=P)
    z_dram = nc.dram_tensor("z_scratch", (BATCH, P, NK, T), F32, kind="Internal").ap()
    o_dram = nc.dram_tensor("o_scratch", (BATCH, T, C), F32, kind="Internal").ap()
    o_v = o_dram.rearrange("b (t p) c -> b p t c", p=P)

    ctx = ExitStack()
    with ctx:
        def sb(name, shape, dt=F32):
            return ctx.enter_context(nc.sbuf_tensor(name, shape, dt))

        def sem(name):
            return ctx.enter_context(nc.semaphore(name))

        with ExitStack() as shared:
            gb = shared.enter_context(nc.sbuf_tensor("gb", [P, NK, T], F32))
            xb = shared.enter_context(nc.sbuf_tensor("xb", [P, NK, T], F32))
        with ExitStack() as shared:
            ob = shared.enter_context(nc.sbuf_tensor("ob", [P, KB, C], F32))
        k_hl, k_h1, q_hh, q_lm = [], [], [], []
        for s in range(2):
            k_hl.append(sb(f"k_hl{s}", [P, T], F32R))
            k_h1.append(sb(f"k_h1{s}", [P, T], F32R))
            q_hh.append(sb(f"q_hh{s}", [P, T], F32R))
            q_lm.append(sb(f"q_lm{s}", [P, T], F32R))
        xh = sb("xh", [P, NK, T], F32R)
        xl = sb("xl", [P, NK, T], F32R)
        v_hl = sb("v_hl", [P, 2, KB, P], F32R)
        vt = sb("vt", [P, T])
        probs = sb("probs", [P, 2, 2 * W])
        with ExitStack() as shared:
            sq1 = shared.enter_context(nc.sbuf_tensor("sq1", [P, NK, W], F32))
        ph = sb("ph", [P, 2, 2 * W], F32R)
        pl = sb("pl", [P, 2, 2 * W], F32R)
        acc = sb("acc", [P, 2, W])
        wq_raw = sb("wq_raw", [P, NK, P])
        w_halves = sb("w_halves", [P, 4, NK, P], F32R)
        wv_raw = sb("wv_raw", [P, NK, P])
        wq_h, wq_l, wv_h, wv_l = (w_halves[:, i, :, :] for i in range(4))
        b_qk = sb("b_qk", [P, 1])
        b_v = sb("b_v", [P, 1])
        ot = sb("ot", [P, W])
        rs = sb("rs", [P, 2, W])
        o_st = sb("o_st", [P, 2, 4, DH])
        nm4 = sb("nm4", [P, 2, 4, NT])
        nm = sb("nm", [P, 2, 4])
        nm_t = sb("nm_t", [4, 2, P], F32R)
        rden = sb("rden", [P, 4])
        carrier = sb("carrier", [P, 1])
        ident = sb("ident", [P, P])
        fold = sb("fold", [P, DH])
        ones = sb("ones", [P, 1])
        zero = sb("zero", [P, 1])
        avg_c = sb("avg_c", [P, P])
        avg_g = sb("avg_g", [P, P])
        par = sb("par", [P, 5, NK])
        bias_y = sb("bias_y", [P, NK])
        bn = sb("bn", [P, NK, NT, 6])
        mv = sb("mv", [P, NK, 2])
        gm = sb("gm", [P, NK])
        gv = sb("gv", [P, NK])
        gs = sb("gs", [P, NK])
        rstd = sb("rstd", [P, KB])
        bn2 = sb("bn2", [P, KB, 6])
        mv2 = sb("mv2", [P, KB, 2])
        rs2 = sb("rs2", [P, KB])
        sq = [probs[:, :, :].rearrange("p a (k w) -> p (a k) w", w=W),
              sq1[:, :, :]]
        diag = [acc[:, 0, :], acc[:, 1, :], rs[:, 0, :], rs[:, 1, :]]
        on_st = [rs[:, 0, :], rs[:, 1, :]]
        wo_raw = vt[:, :].rearrange("p (k w) -> p k w", w=W)
        wo_h = v_hl[:, 0, :, :].rearrange("p t c -> p (t c)").rearrange("p (k w) -> p k w", w=W)
        wo_l = w_halves[:, :, :, :].rearrange("p a k c -> p a (k c)")
        z_st = vt[:, :].rearrange("p (k w) -> p k w", w=W)

        ps = ctx.enter_context(nc.psum_tensor("ps", [P, 8, W], F32))

        const_set, const_ready, fold_ready, par_in = sem("const_set"), sem("const_ready"), sem("fold_ready"), sem("par_in")
        bias_ready = sem("bias_ready")
        sq_half, sq_sum = sem("sq_half"), sem("sq_sum")
        x_in = [sem(f"x_in{k}") for k in range(NK)]
        bn_done, bn_agg = sem("bn_done"), sem("bn_agg")
        gn_in, gn_sum, gn_dve, gn_std = sem("gn_in"), sem("gn_sum"), sem("gn_dve"), sem("gn_std")
        g_ready, mean_ready, dev_ready, sq_ready = sem("g_ready"), sem("mean_ready"), sem("dev_ready"), sem("sq_ready")
        var_ready, veps_ready, std_ready, inv_ready = sem("var_ready"), sem("veps_ready"), sem("std_ready"), sem("inv_ready")
        diag_ready, spread_ready = sem("diag_ready"), sem("spread_ready")
        norm_ready, xh_ready, xl_ready = sem("norm_ready"), sem("xh_ready"), sem("xl_ready")
        z_ready, z_out, rows_set = sem("z_ready"), sem("z_out"), sem("rows_set")
        wq_in, wq_hi, wq_lo = sem("wq_in"), sem("wq_hi"), sem("wq_lo")
        wv_in, wv_hi, wv_lo = sem("wv_in"), sem("wv_hi"), sem("wv_lo")
        qk_full, qk_hi, qk_lo, dup_in = sem("qk_full"), sem("qk_hi"), sem("qk_lo"), sem("dup_in")
        v_full, vt_ready, turn_full, v_hi, v_lo = sem("v_full"), sem("vt_ready"), sem("turn_full"), sem("v_hi"), sem("v_lo")
        mx_full, mx_free = sem("mx_full"), [sem("mx_free0"), sem("mx_free1")]
        nm_ready, nm_full, nm_t_ready = sem("nm_ready"), sem("nm_full"), sem("nm_t_ready")
        row_in = [sem(f"row_in{q}") for q in range(NT)]
        s_ready, e_ready, ph_ready, pl_ready = sem("s_ready"), sem("e_ready"), sem("ph_ready"), sem("pl_ready")
        acc_step, acc_ready, pv_done = sem("acc_step"), sem("acc_ready"), sem("pv_done")
        fold_full = sem("fold_full")
        ot_ready, rden_ready, o_ready, o_out = sem("ot_ready"), sem("rden_ready"), sem("o_ready"), [sem("o_out0"), sem("o_out1")]
        ob_in = [sem(f"ob_in{t}") for t in range(NT)]
        wo_in, wo_hi, wo_lo = sem("wo_in"), sem("wo_hi"), sem("wo_lo")
        bn2_done, mv2_done, ve2_ready, std2_ready, inv2_ready = (sem("bn2_done"), sem("mv2_done"), sem("ve2_ready"),
                                                                 sem("std2_ready"), sem("inv2_ready"))
        on_ready, tr_ready, aff_ready, onh_ready, onl_ready = (sem("on_ready"), sem("tr_ready"), sem("aff_ready"),
                                                               sem("onh_ready"), sem("onl_ready"))
        po_ready, y_ready = sem("po_ready"), sem("y_ready")
        z_in = [sem(f"z_in{i}") for i in range(4)]
        y_out = [sem(f"y_out{i}") for i in range(4)]

        block = ctx.enter_context(nc.Block())

        @block.sync
        def _(sp):
            with nc.allow_non_contiguous_dma(reason="per-channel parameters"):
                for i, v in enumerate((gamma1, beta1, gamma2, beta2, b_out)):
                    sp.dma_start(par[:, i, :], v.rearrange("(k p) -> p k", p=P)).then_inc(par_in, 16)

            def load_qk_weights(b_h, h):
                sp.wait_ge(qk_lo, h * NT)
                sp.wait_ge(wq_lo, h)
                for i in range(2):
                    col = b_h * DH + i * C
                    sp.dma_start(wq_raw[:, :, i * DH:(i + 1) * DH], w_v[:, :, bass.ds(col, DH)]).then_inc(wq_in, 16)
                    sp.dma_start(b_qk[i * DH:(i + 1) * DH, :],
                                 b_qkv[bass.ds(col, DH)].rearrange("(p o) -> p o", o=1)).then_inc(wq_in, 16)

            def load_v_weights(b_p, pair):
                sp.wait_ge(vt_ready, pair * NT)
                sp.wait_ge(wv_lo, pair)
                col = b_p * P + 2 * C
                sp.dma_start(wv_raw[:, :, :], w_v[:, :, bass.ds(col, P)]).then_inc(wv_in, 16)
                sp.dma_start(b_v[:, :], b_qkv[bass.ds(col, P)].rearrange("(p o) -> p o", o=1)).then_inc(wv_in, 16)

            def duplicate(h, s, t):
                sp.wait_ge(qk_hi, h * NT + t + 1)
                w = slice(t * W, (t + 1) * W)
                sp.dma_start(q_hh[s][DH:P, w].bitcast(F32), q_hh[s][0:DH, w].bitcast(F32)).then_inc(dup_in, 16)
                sp.dma_start(k_h1[s][0:DH, w].bitcast(F32), k_hl[s][0:DH, w].bitcast(F32)).then_inc(dup_in, 16)

            def max_row(h, s, q):
                sp.wait_ge(nm_t_ready, h * NT + q + 1)
                sp.dma_start(q_lm[s][DH:DH + 1, q * W:(q + 1) * W].bitcast(F32).rearrange("o (a b) -> o a b", a=4),
                             nm_t[:, q % 2, :].bitcast(F32)).then_inc(row_in[q], 16)

            def store_heads(b, b_h, h, q):
                sp.wait_ge(o_ready, h * NT + q + 1)
                sp.dma_start(o_v[bass.ds(b, 1), :, q * 4:(q + 1) * 4, bass.ds(b_h * DH, DH)].rearrange("o p t c -> (o p) t c"),
                             o_st[:, q % 2, :, :]).then_inc(o_out[q % 2], 16)

            def beside_last(b, slot, u):
                if u == LOAD_WO:
                    sp.wait_ge(turn_full, slot.h * NT + NT)
                    sp.dma_start(wo_raw, wo_v).then_inc(wo_in, 16)
                if u == LOAD_OB:
                    sp.wait_ge(pv_done, slot.units)
                    for i in range(2):
                        sp.wait_ge(o_out[i], slot.stores)
                    for t in range(NT):
                        sp.dma_start(ob[:, t * 4:(t + 1) * 4, 0:C - DH],
                                     o_v[bass.ds(b, 1), :, t * 4:(t + 1) * 4, 0:C - DH].rearrange("o p t c -> (o p) t c")
                                     ).then_inc(ob_in[t], 16)
                if u == LOAD_Z:
                    sp.wait_ge(wo_lo, b * NK + NK)
                    sp.wait_ge(z_out, b * (16 * NT) + 16 * NT)
                    for c in range(NK):
                        load_z(b, 0, c)

            def load_z(b, t, c):
                sp.dma_start(z_st[:, c, :],
                             z_dram[bass.ds(b, 1), :, c, t * W:(t + 1) * W].rearrange("o p t -> (o p) t")).then_inc(z_in[c], 16)

            def load_x(b, ahead):
                for k in range(NK):
                    sp.dma_start(xb[:, k, :], x_v[bass.ds(b + ahead, 1), :, k, :].rearrange("o p t -> (o p) t")).then_inc(x_in[k], 16)

            load_x(0, 0)

            def beside(b, p, slot, u):
                s, b_h = slot.odd, p * 2 + slot.odd
                if not slot.has_next:
                    beside_last(b, slot, u)
                if u in FOLD and not (slot.first and u == LAG) and (slot.has_next or FOLD[u] < 0):
                    q = FOLD[u]
                    store_heads(b, b_h + (-1 if q < 0 else 0), slot.h + (-1 if q < 0 else 0), q % NT)
                if u == LOAD_WEIGHTS and slot.has_pair:
                    load_qk_weights(b_h + 2, slot.h + 2)
                    if not slot.odd:
                        load_v_weights(p + 1, slot.pair + 1)
                t = ended(QK_PROJ, u)
                if t is not None and slot.has_next:
                    duplicate(slot.h + 1, 1 - s, t)
                if u in NM_TURN:
                    ahead, q = divmod(NM_TURN[u], NT)
                    if not ahead or slot.has_next:
                        max_row(slot.h + ahead, s ^ ahead, q)

            def batch(b, final=False):
                load_qk_weights(0, b * HEADS)
                load_v_weights(0, b * (HEADS // 2))
                for t in range(NT):
                    w = slice(t * W, (t + 1) * W)
                    sp.wait_ge(z_ready, b * NT + t + 1)
                    sp.dma_start(z_dram[bass.ds(b, 1), :, :, w].rearrange("o p k t -> (o p) k t"), xb[:, :, w]).then_inc(z_out, 16)
                for t in range(NT):
                    duplicate(b * HEADS, 0, t)
                load_qk_weights(1, b * HEADS + 1)
                h, units = b * HEADS, opening(b)
                sp.wait_ge(rows_set, b * 4 + 2)
                max_row(h, 0, 0)
                for slot, u in units:
                    beside(b, 0, slot, u)
                with sp.Fori(0, HEADS // 2 - 1) as p:
                    for i, (slot, u) in enumerate(turn(b, p)):
                        beside(b, p if i < 2 * UNITS - OPEN else p + 1, slot, u)
                for slot, u in turn(b, HEADS // 2 - 1, last_pair=True):
                    beside(b, HEADS // 2 - 1, slot, u)
                if not final:
                    sp.wait_ge(pv_done, b * (HEADS * UNITS) + HEADS * UNITS)
                    load_x(b, 1)

                def store_y(t, c):
                    n = t * NK + c
                    sp.wait_ge(y_ready, b * (NT * NK) + n + 1)
                    sp.dma_start(out_v[bass.ds(b, 1), :, c, t * W:(t + 1) * W].rearrange("o p t -> (o p) t"),
                                 z_st[:, c, :]).then_inc(y_out[c], 16)

                for t in range(NT):
                    for c in range(NK):
                        store_y(t, c)
                        if t + 1 < NT:
                            sp.wait_ge(y_out[c], b * (16 * NT) + 16 * (t + 1))
                            load_z(b, t + 1, c)

            with sp.Fori(0, BATCH - 1) as b:
                batch(b)
            batch(BATCH - 1, final=True)
            for c in range(NK):
                sp.wait_ge(y_out[c], BATCH * 16 * NT)

        @block.gpsimd
        def _(pool):
            for tile, value in ((ident, 0.0), (zero, 0.0), (ones, 1.0), (avg_c, 1.0 / C), (avg_g, 1.0 / GROUP)):
                nc.gpsimd.memset(tile[:, :], value).then_inc(const_set, 1)
            pool.wait_ge(const_set, 5)
            nc.gpsimd.affine_select(out=ident[:, :], in_=ident[:, :], compare_op=ALU.not_equal, fill=1.0, base=0,
                                    pattern=[[-1, P]], channel_multiplier=1).then_inc(const_ready, 1)
            groups = avg_g[:, :].rearrange("p (g i) -> p g i", i=GROUP)
            nc.gpsimd.affine_select(out=groups, in_=groups, compare_op=ALU.is_ge, fill=0.0, base=0,
                                    pattern=[[-GROUP, P // GROUP], [0, GROUP]], channel_multiplier=1).then_inc(const_set, 1)
            pool.wait_ge(const_set, 6)
            nc.gpsimd.affine_select(out=groups, in_=groups, compare_op=ALU.is_ge, fill=0.0, base=GROUP - 1,
                                    pattern=[[GROUP, P // GROUP], [0, GROUP]], channel_multiplier=-1).then_inc(const_ready, 1)

            def unit(slot, u):
                q, j = divmod(u, UPB)
                pool.wait_ge(e_ready, slot.units * 2 + (2 * u + 2))
                two = [probs[:, u % 2, i * W:(i + 1) * W] for i in range(2)]
                if j == 0:
                    if q > 1 or not slot.first:
                        pool.wait_ge(fold_full, slot.h * NT + (q - 1))
                    nc.gpsimd.tensor_tensor(acc[:, q % 2, :], two[0], two[1], ALU.add).then_inc(acc_ready, 1)
                else:
                    pool.wait_ge(acc_ready, slot.units + u)
                    nc.gpsimd.tensor_tensor(acc[:, q % 2, :], acc[:, q % 2, :], two[0], ALU.add).then_inc(acc_step, 1)
                    pool.wait_ge(acc_step, slot.h * (UNITS - NT) + (u - q))
                    nc.gpsimd.tensor_tensor(acc[:, q % 2, :], acc[:, q % 2, :], two[1], ALU.add).then_inc(acc_ready, 1)

            def sum_squares(b, ahead, t):
                pool.wait_ge(sq_ready, b * NT + (ahead * NT + t + 1))
                q = sq[t % 2]
                nc.gpsimd.tensor_tensor(q[:, 0:2, :], q[:, 0:2, :], q[:, 2:4, :], ALU.add).then_inc(sq_half, 1)
                pool.wait_ge(sq_half, b * NT + (ahead * NT + t + 1))
                nc.gpsimd.tensor_tensor(q[:, 0, :], q[:, 0, :], q[:, 1, :], ALU.add).then_inc(sq_sum, 1)

            def add_x(b, t):
                w = slice(t * W, (t + 1) * W)
                pool.wait_ge(norm_ready, b * NT + t + 1)
                nc.gpsimd.tensor_tensor(xb[:, :, w], xb[:, :, w], gb[:, :, w], ALU.add).then_inc(z_ready, 1)

            for t in range(3):
                sum_squares(0, 0, t)

            def batch(b, final=False):
                add_x(b, 0)
                sum_squares(b, 0, 3)
                for t in range(1, NT):
                    add_x(b, t)
                for s in range(2):
                    if s == 0:
                        pool.wait_ge(z_ready, (b + 1) * NT)
                        pool.wait_ge(xl_ready, (b + 1) * NT)
                    else:
                        pool.wait_ge(z_out, (b + 1) * (16 * NT))
                    zeros, one = (c[DH:P, 0:1].to_broadcast([P - DH, T]) for c in (zero, ones))
                    nc.gpsimd.tensor_tensor(k_h1[s][DH:P, :], one, zeros, ALU.add).then_inc(rows_set, 1)
                    nc.gpsimd.tensor_tensor(q_lm[s][DH:P, :], zeros, zeros, ALU.add).then_inc(rows_set, 1)
                for slot, u in opening(b):
                    unit(slot, u)
                with pool.Fori(0, HEADS // 2 - 1) as p:
                    for slot, u in turn(b, p):
                        unit(slot, u)
                for slot, u in turn(b, HEADS // 2 - 1, last_pair=True):
                    unit(slot, u)
                if not final:
                    for t in range(3):
                        sum_squares(b, 1, t)

            with pool.Fori(0, BATCH - 1) as b:
                batch(b)
            batch(BATCH - 1, final=True)

        @block.scalar
        def _(act):
            def split_qk(h):
                act.wait_ge(wq_in, h * 64 + 64)
                act.wait_ge(qk_full, h * NT)
                nc.scalar.activation(wq_h[:, :, :], wq_raw[:, :, :], ACT.Copy).then_inc(wq_hi, 1)

            def split_v(pair):
                act.wait_ge(wv_in, pair * 32 + 32)
                act.wait_ge(v_full, pair * NT)
                nc.scalar.activation(wv_h[:, :, :], wv_raw[:, :, :], ACT.Copy).then_inc(wv_hi, 1)

            def qk_halves(h, s, t, free, bank=BANK_PROJ):
                act.wait_ge(pv_done, free)
                act.wait_ge(qk_full, h * NT + (t + 1))
                w = slice(t * W, (t + 1) * W)
                nc.scalar.activation(q_hh[s][0:DH, w], ps[0:DH, bank, :], ACT.Identity, bias=b_qk[0:DH, :])
                nc.scalar.activation(k_hl[s][0:DH, w], ps[DH:P, bank, :], ACT.Identity,
                                     bias=b_qk[DH:P, :]).then_inc(qk_hi, 1)

            def v_rows(pair, t, bank=BANK_PROJ):
                act.wait_ge(v_full, pair * NT + (t + 1))
                nc.scalar.activation(vt[:, t * W:(t + 1) * W], ps[:, bank, :], ACT.Identity,
                                     bias=b_v[:, :]).then_inc(vt_ready, 1)

            def v_halves(h, s, t, free, bank=BANK_PROJ):
                act.wait_ge(turn_full, h * NT + (t + 1))
                act.wait_ge(pv_done, free)
                src = ps[:, bank, :].rearrange("p (t c) -> p t c", c=P)[:, :, s * DH:(s + 1) * DH]
                nc.scalar.activation(v_hl[:, s, t * 4:(t + 1) * 4, 0:DH], src, ACT.Copy).then_inc(v_hi, 1)

            def max_columns(h, q):
                act.wait_ge(nm_full, h * NT + (q + 1))
                act.wait_ge(row_in[(q + 2) % NT], h * 16 if q < 2 else h * 16 + 16)
                nc.scalar.activation(nm_t[:, q % 2, :], ps[0:4, BANK_MISC, 0:P], ACT.Copy).then_inc(nm_t_ready, 1)

            def take_output(slot, q):
                act.wait_ge(pv_done, slot.units + (q + 1) * UPB)
                act.wait_ge(fold_full, slot.h * NT + q)
                nc.scalar.activation(ot[:, :], ps[:, BANK_PV, :], ACT.Copy).then_inc(ot_ready, 1)

            def unit(slot, u):
                s = slot.odd
                if u in FOLD and not (slot.first and u == LAG):
                    take_output(slot, FOLD[u])
                t = ended(QK_PROJ, u)
                if t is not None and slot.has_next:
                    qk_halves(slot.h + 1, 1 - s, t, slot.units)
                t = ended(V_PROJ[s], u)
                if t is not None and slot.has_pair:
                    v_rows(slot.pair + 1, t)
                if u - 1 in V_TURN[slot.odd] and slot.has_next:
                    v_halves(slot.h + 1, 1 - s, V_TURN[slot.odd][u - 1], slot.units)
                if u - 1 in NM_TURN:
                    ahead, q = divmod(NM_TURN[u - 1], NT)
                    if not ahead or slot.has_next:
                        max_columns(slot.h + ahead, q)
                if u == SPLIT_QK and slot.has_pair:
                    split_qk(slot.h + 2)
                if u == SPLIT_V and slot.has_pair and not slot.odd:
                    split_v(slot.pair + 1)
                act.wait_ge(pl_ready, slot.two_before(u))
                act.wait_ge(acc_ready, slot.two_before(u))
                for i in range(2):
                    act.wait_ge(s_ready, slot.units * 2 + (2 * u + i + 1))
                    e = nc.scalar.activation(probs[:, u % 2, i * W:(i + 1) * W], ps[:, BANK_S[(2 * u + i + 64 * s) % 3], :],
                                             ACT.Exp, scale=SCALE).then_inc(e_ready, 1)
                act.wait_ge(e_ready, slot.units * 2 + (2 * u + 2))
                act.wait_ge(pv_done, slot.two_before(u))
                nc.scalar.activation(ph[:, u % 2, :], probs[:, u % 2, :], ACT.Copy).then_inc(ph_ready, 1)

            def group_std(b, ahead):
                act.wait_ge(gn_dve, b * 4 + (4 * ahead + 3))
                nc.scalar.activation(gs[:, :], gv[:, :], ACT.Sqrt).then_inc(gn_std, 1)

            def output_std(b, t):
                act.wait_ge(ve2_ready, b * NT + t + 1)
                nc.scalar.activation(rs2[:, t * 4:(t + 1) * 4], rs2[:, t * 4:(t + 1) * 4], ACT.Sqrt).then_inc(std2_ready, 1)

            def output_hi(b, t, k):
                n = t * NK + k
                act.wait_ge(tr_ready, b * (NT * NK) + n + 1)
                if n > 1:
                    act.wait_ge(onl_ready, b * (NT * NK) + n - 1)
                nc.scalar.activation(on_st[n % 2], ps[:, BANK_TURN, :], ACT.Identity, scale=par[:, 2, k:k + 1],
                                     bias=par[:, 3, k:k + 1]).then_inc(aff_ready, 1)
                act.wait_ge(aff_ready, b * (NT * NK) + n + 1)
                nc.scalar.activation(xh[:, k, t * W:(t + 1) * W], on_st[n % 2], ACT.Copy).then_inc(onh_ready, 1)

            def beside_last(b, u):
                if u in SPLIT_WO:
                    k = SPLIT_WO[u]
                    act.wait_ge(wo_in, b * 16 + 16)
                    nc.scalar.activation(wo_h[:, k, :], wo_raw[:, k, :], ACT.Copy).then_inc(wo_hi, 1)
                if u == OUT_STD:
                    for t in range(OUT_EARLY):
                        output_std(b, t)

            def squares(b, ahead, t):
                act.wait_ge(dev_ready, b * NT + (ahead * NT + t + 1))
                if t > 1:
                    act.wait_ge(var_ready, b * NT + (ahead * NT + t - 1))
                nc.scalar.activation(sq[t % 2], gb[:, :, t * W:(t + 1) * W], ACT.Square).then_inc(sq_ready, 1)

            def layer_std(b, ahead, t):
                r = rstd[:, 4 * t:4 * t + 4]
                act.wait_ge(veps_ready, b * NT + (ahead * NT + t + 1))
                nc.scalar.activation(r, r, ACT.Sqrt, scale=1.0 / C ** 2).then_inc(std_ready, 1)

            def xn_hi(b, t):
                act.wait_ge(norm_ready, b * NT + t + 1)
                w = slice(t * W, (t + 1) * W)
                for k in range(NK):
                    hi = nc.scalar.activation(xh[:, k, w], gb[:, k, w], ACT.Identity, bias=par[:, 1, k:k + 1])
                hi.then_inc(xh_ready, 1)

            def norm_first(b, ahead):
                group_std(b, ahead)
                squares(b, ahead, 0)
                squares(b, ahead, 1)
                layer_std(b, ahead, 0)
                squares(b, ahead, 2)
                layer_std(b, ahead, 1)

            act.wait_ge(par_in, 80)
            norm_first(0, 0)

            def batch(b, final=False):
                act.wait_ge(po_ready, b * (NT * NK))
                xn_hi(b, 0)
                squares(b, 0, 3)
                split_qk(b * HEADS)
                layer_std(b, 0, 2)
                xn_hi(b, 1)
                split_v(b * (HEADS // 2))
                layer_std(b, 0, 3)
                xn_hi(b, 2)
                xn_hi(b, 3)
                for t in range(NT):
                    act.wait_ge(z_ready, b * NT + t + 1)
                    act.wait_ge(xl_ready, b * NT + t + 1)
                    qk_halves(b * HEADS, 0, t, b * (HEADS * UNITS), bank=t)
                for t in range(NT):
                    v_rows(b * (HEADS // 2), t, bank=4 + t)
                for t in range(NT):
                    v_halves(b * HEADS, 0, t, b * (HEADS * UNITS), bank=t)
                act.wait_ge(rows_set, (b + 1) * 4)
                max_columns(b * HEADS, 0)
                split_qk(b * HEADS + 1)
                for slot, u in opening(b):
                    unit(slot, u)
                with act.Fori(0, HEADS // 2 - 1) as p:
                    for slot, u in turn(b, p):
                        unit(slot, u)
                for slot, u in turn(b, HEADS // 2 - 1, last_pair=True):
                    if not slot.has_next and u - 1 in OUT_TURN:
                        output_hi(b, *OUT_TURN[u - 1])
                    unit(slot, u)
                    if not slot.has_next:
                        beside_last(b, u)
                take_output(Slot(b + 1, 0, 0), -1)
                output_std(b, 2)
                for n in range(2 * NK, NT * NK):
                    if n == 2 * NK + 2:
                        output_std(b, 3)
                    output_hi(b, *divmod(n, NK))
                if not final:
                    norm_first(b, 1)

            with act.Fori(0, BATCH - 1) as b:
                batch(b)
            batch(BATCH - 1, final=True)

        @block.vector
        def _(dve):
            def split_qk(h):
                dve.wait_ge(wq_hi, h + 1)
                nc.vector.tensor_tensor(wq_l[:, :, :], wq_raw[:, :, :], wq_h[:, :, :], ALU.subtract).then_inc(wq_lo, 1)

            def split_v(pair):
                dve.wait_ge(wv_hi, pair + 1)
                nc.vector.tensor_tensor(wv_l[:, :, :], wv_raw[:, :, :], wv_h[:, :, :], ALU.subtract).then_inc(wv_lo, 1)

            def qk_remainders(h, s, t, bank=BANK_PROJ):
                dve.wait_ge(qk_hi, h * NT + t + 1)
                w = slice(t * W, (t + 1) * W)
                nc.vector.scalar_tensor_tensor(out=q_lm[s][0:DH, w], in0=ps[0:DH, bank, :], scalar=b_qk[0:DH, :],
                                               in1=q_hh[s][0:DH, w], op0=ALU.add, op1=ALU.subtract)
                nc.vector.scalar_tensor_tensor(out=k_hl[s][DH:P, w], in0=ps[DH:P, bank, :], scalar=b_qk[DH:P, :],
                                               in1=k_hl[s][0:DH, w], op0=ALU.add, op1=ALU.subtract).then_inc(qk_lo, 1)

            def v_remainders(h, s, t, bank=BANK_PROJ):
                dve.wait_ge(v_hi, h * NT + t + 1)
                src = ps[:, bank, :].rearrange("p (t c) -> p t c", c=P)[:, :, s * DH:(s + 1) * DH]
                nc.vector.tensor_tensor(v_hl[:, s, t * 4:(t + 1) * 4, DH:P], src, v_hl[:, s, t * 4:(t + 1) * 4, 0:DH],
                                        ALU.subtract).then_inc(v_lo, 1)

            def reduce_max(h, q, step, base, half, n):
                dve.wait_ge(mx_full, base + (n + 1))
                i, kc = divmod(step, NT)
                nc.vector.tensor_reduce(nm4[:, q % 2, i, kc:kc + 1], ps[:, BANK_MX[n % 2], :], op=ALU.max, axis=AX.X,
                                        negate=True).then_inc(mx_free[n % 2], 1)
                if step == 4 * NT - 1:
                    for parity in range(2):
                        dve.wait_ge(mx_free[parity], half + (n + 2 - parity) // 2)
                    nc.vector.tensor_reduce(nm[:, q % 2, :], nm4[:, q % 2, :, :], op=ALU.min, axis=AX.X).then_inc(nm_ready, 1)

            def take_fold(h, q, stores, direct=False):
                dve.wait_ge(fold_full, h * NT + (q + 1))
                src = ps[:, BANK_MISC, 0:4 * (DH + 1)].rearrange("p (t c) -> p t c", c=DH + 1)
                nc.vector.reciprocal(rden[:, :], src[:, :, DH]).then_inc(rden_ready, 1)
                dve.wait_ge(rden_ready, h * NT + (q + 1))
                if not direct:
                    dve.wait_ge(o_out[q % 2], stores + 16 * (q // 2))
                dest = ob[:, q * 4:(q + 1) * 4, C - DH:C] if direct else o_st[:, q % 2, :, :]
                nc.vector.tensor_tensor(dest, src[:, :, 0:DH],
                                        rden[:, :].rearrange("p (t o) -> p t o", o=1).to_broadcast([P, 4, DH]),
                                        ALU.mult).then_inc(o_ready, 1)

            def output_stats(b, t, half):
                if half == 0:
                    dve.wait_ge(ob_in[t], b * 16 + 16)
                    dve.wait_ge(o_ready, b * (HEADS * NT) + ((HEADS - 1) * NT + t + 1))
                for i in range(4 * t + 2 * half, 4 * t + 2 * half + 2):
                    nc.vector.bn_stats(bn2[:, i, :], ob[:, i, :]).then_inc(bn2_done, 1)
                if half == 0:
                    return
                dve.wait_ge(bn2_done, b * KB + 4 * t + 4)
                nc.vector.memset(carrier[:, :], 0.0)
                for i in range(4 * t, 4 * t + 4):
                    nc.vector.bn_aggr(mv2[:, i, :], bn2[:, i, :]).then_inc(mv2_done, 1)
                dve.wait_ge(mv2_done, b * KB + 4 * t + 4)
                nc.vector.tensor_scalar(rs2[:, 4 * t:4 * t + 4], mv2[:, 4 * t:4 * t + 4, 1], EPS, None,
                                        ALU.add).then_inc(ve2_ready, 1)

            def output_norm(b, t):
                r = rs2[:, 4 * t:4 * t + 4]
                dve.wait_ge(std2_ready, b * NT + t + 1)
                nc.vector.reciprocal(r, r).then_inc(inv2_ready, 1)
                dve.wait_ge(inv2_ready, b * NT + t + 1)
                for i in range(4 * t, 4 * t + 4):
                    on = nc.vector.tensor_scalar(ob[:, i, :], ob[:, i, :], mv2[:, i, 0:1], rs2[:, i:i + 1],
                                                 ALU.subtract, ALU.mult)
                on.then_inc(on_ready, 1)

            def output_lo(b, t, k):
                n = t * NK + k
                dve.wait_ge(onh_ready, b * (NT * NK) + n + 1)
                nc.vector.tensor_tensor(xl[:, k, t * W:(t + 1) * W], on_st[n % 2], xh[:, k, t * W:(t + 1) * W],
                                        ALU.subtract).then_inc(onl_ready, 1)

            def residual(b, t, c):
                n = t * NK + c
                dve.wait_ge(po_ready, b * (NT * NK) + n + 1)
                dve.wait_ge(z_in[c], b * (16 * NT) + 16 * (t + 1))
                nc.vector.scalar_tensor_tensor(out=z_st[:, c, :], in0=ps[:, BANK_OUT[n % 2], :], scalar=bias_y[:, c:c + 1],
                                               in1=z_st[:, c, :], op0=ALU.add, op1=ALU.add).then_inc(y_ready, 1)

            def beside_last(b, u):
                if u in SPLIT_WO:
                    k = SPLIT_WO[u]
                    dve.wait_ge(wo_hi, b * NK + k + 1)
                    nc.vector.tensor_tensor(wo_l[:, k, :], wo_raw[:, k, :], wo_h[:, k, :], ALU.subtract).then_inc(wo_lo, 1)
                if u in OUT_STATS:
                    output_stats(b, *OUT_STATS[u])
                if u in OUT_NORM:
                    output_norm(b, OUT_NORM[u])
                if u - 1 in OUT_TURN:
                    output_lo(b, *OUT_TURN[u - 1])

            def channel_stats(b, ahead, k):
                dve.wait_ge(x_in[k], b * 16 + (ahead * 16 + 16))
                for t in range(NT):
                    nc.vector.bn_stats(bn[:, k, t, :], xb[:, k, t * W:(t + 1) * W]).then_inc(bn_done, 1)

            def channel_moments(b, ahead):
                dve.wait_ge(bn_done, b * (NK * NT) + (ahead + 1) * (NK * NT))
                nc.vector.memset(carrier[:, :], 0.0)
                for k in range(NK):
                    nc.vector.bn_aggr(mv[:, k, :], bn[:, k, :, :]).then_inc(gn_in if k == NK - 1 else bn_agg, 1)

            def group_moments(b, ahead):
                dve.wait_ge(gn_sum, b * 2 + (ahead * 2 + 1))
                nc.vector.tensor_copy(gm[:, :], ps[:, BANK_MISC, 0:NK]).then_inc(gn_dve, 1)
                dve.wait_ge(gn_dve, b * 4 + (ahead * 4 + 1))
                nc.vector.tensor_tensor(gv[:, :], mv[:, :, 0], gm[:, :], ALU.subtract).then_inc(bn_agg, 1)
                dve.wait_ge(bn_agg, b * (NK + 1) + (ahead * (NK + 1) + NK))
                nc.vector.tensor_tensor(gv[:, :], gv[:, :], gv[:, :], ALU.mult).then_inc(bn_agg, 1)
                dve.wait_ge(bn_agg, b * (NK + 1) + (ahead * (NK + 1) + NK + 1))
                nc.vector.tensor_tensor(gs[:, :], gv[:, :], mv[:, :, 1], ALU.add).then_inc(gn_dve, 1)

            def group_variance(b, ahead):
                dve.wait_ge(gn_sum, b * 2 + (ahead * 2 + 2))
                nc.vector.tensor_scalar(gv[:, :], ps[:, BANK_MISC, 0:NK], EPS, None, ALU.add).then_inc(gn_dve, 1)

            def group_scale(b, ahead):
                dve.wait_ge(gn_std, b + (ahead + 1))
                nc.vector.reciprocal(gs[:, :], gs[:, :]).then_inc(gn_dve, 1)

            def group_norm(b, ahead, k):
                dve.wait_ge(gn_dve, b * 4 + (ahead * 4 + 4))
                nc.vector.tensor_scalar(gb[:, k, :], xb[:, k, :], gm[:, k:k + 1], gs[:, k:k + 1], ALU.subtract,
                                        ALU.mult).then_inc(g_ready, 1)

            def unit(slot, u):
                s = slot.odd
                if u - 1 in FOLD and not (slot.first and u - 1 == LAG):
                    q = FOLD[u - 1]
                    if q < 0:
                        take_fold(slot.h - 1, NT - 1, slot.stores - 16 * NT // 2)
                    else:
                        take_fold(slot.h, q, slot.stores, direct=not slot.has_next)
                t = ended(QK_PROJ, u)
                if t is not None and slot.has_next:
                    qk_remainders(slot.h + 1, 1 - s, t)
                if u - 1 in V_TURN[slot.odd] and slot.has_next:
                    v_remainders(slot.h + 1, 1 - s, V_TURN[slot.odd][u - 1])
                if u == SPLIT_QK and slot.has_pair:
                    split_qk(slot.h + 2)
                if u == SPLIT_V and slot.has_pair and not slot.odd:
                    split_v(slot.pair + 1)
                for i, (ahead, q, step) in enumerate(max_steps(slot, u)):
                    reduce_max(slot.h + ahead, q, step, slot.mx, slot.mx_half, 2 * u + i)
                dve.wait_ge(ph_ready, slot.units + (u + 1))
                dve.wait_ge(pv_done, slot.two_before(u))
                nc.vector.tensor_tensor(pl[:, u % 2, :], probs[:, u % 2, :], ph[:, u % 2, :],
                                        ALU.subtract).then_inc(pl_ready, 1)

            dve.wait_ge(par_in, 80)
            dve.wait_ge(const_ready, 1)
            nc.vector.tensor_tensor(fold[:, :], ident[:, 0:DH], ident[:, DH:P], ALU.add).then_inc(fold_ready, 1)
            nc.vector.tensor_tensor(bias_y[:, :], par[:, 1, :], par[:, 4, :], ALU.add).then_inc(bias_ready, 1)
            dve.wait_ge(bias_ready, 1)
            def deviations(b, ahead, t):
                dve.wait_ge(mean_ready, b * NT + (ahead * NT + t + 1))
                w = gb[:, :, t * W:(t + 1) * W]
                mean = ps[:, t:t + 1, :].to_broadcast([P, NK, W])
                nc.vector.tensor_tensor(w, w, mean, ALU.subtract).then_inc(dev_ready, 1)

            def layer_scale(b, ahead, t):
                r = rstd[:, 4 * t:4 * t + 4]
                dve.wait_ge(var_ready, b * NT + (ahead * NT + t + 1))
                nc.vector.tensor_scalar(r, ps[:, BANK_VAR[t % 2], 0:4], EPS, None, ALU.add).then_inc(veps_ready, 1)
                dve.wait_ge(std_ready, b * NT + (ahead * NT + t + 1))
                nc.vector.reciprocal(r, r).then_inc(inv_ready, 1)
                dve.wait_ge(inv_ready, b * NT + (ahead * NT + t + 1))
                nc.vector.tensor_tensor(diag[t].rearrange("p (i c) -> p i c", c=P),
                                        ident[:, :].rearrange("p (o c) -> p o c", o=1).to_broadcast([P, 4, P]),
                                        r.rearrange("p (i o) -> p i o", o=1).to_broadcast([P, 4, P]),
                                        ALU.mult).then_inc(diag_ready, 1)

            def layer_norm(b, ahead, t):
                dve.wait_ge(spread_ready, b * NT + (ahead * NT + t + 1))
                for k in range(NK):
                    w = gb[:, k, t * W:(t + 1) * W]
                    norm = nc.vector.scalar_tensor_tensor(out=w, in0=w, scalar=par[:, 0, k:k + 1], in1=ps[:, BANK_VAR[t % 2], :],
                                                          op0=ALU.mult, op1=ALU.mult)
                norm.then_inc(norm_ready, 1)

            def xn_lo(b, t):
                w = slice(t * W, (t + 1) * W)
                dve.wait_ge(xh_ready, b * NT + t + 1)
                for k in range(NK):
                    lo = nc.vector.scalar_tensor_tensor(out=xl[:, k, w], in0=gb[:, k, w], scalar=par[:, 1, k:k + 1],
                                                        in1=xh[:, k, w], op0=ALU.add, op1=ALU.subtract)
                lo.then_inc(xl_ready, 1)

            for k in range(NK):
                channel_stats(0, 0, k)
            for step in (channel_moments, group_moments, group_variance, group_scale):
                step(0, 0)
            for k in range(NK):
                group_norm(0, 0, k)
            deviations(0, 0, 0)
            deviations(0, 0, 1)
            layer_scale(0, 0, 0)
            deviations(0, 0, 2)
            layer_norm(0, 0, 0)
            layer_scale(0, 0, 1)
            deviations(0, 0, 3)
            layer_norm(0, 0, 1)

            def batch(b, final=False):
                layer_scale(b, 0, 2)
                split_qk(b * HEADS)
                layer_norm(b, 0, 2)
                layer_scale(b, 0, 3)
                xn_lo(b, 0)
                layer_norm(b, 0, 3)
                split_v(b * (HEADS // 2))
                xn_lo(b, 1)
                xn_lo(b, 2)
                xn_lo(b, 3)
                for t in range(NT):
                    dve.wait_ge(z_ready, b * NT + t + 1)
                    qk_remainders(b * HEADS, 0, t, bank=t)
                for n in range(PRO_MX):
                    q, step = divmod(n, 16)
                    reduce_max(b * HEADS, q, step, b * BATCH_MX, b * (BATCH_MX // 2), n)
                    if n - 2 in PRO_TURN:
                        v_remainders(b * HEADS, 0, PRO_TURN[n - 2], bank=PRO_TURN[n - 2])
                split_qk(b * HEADS + 1)
                for slot, u in opening(b):
                    unit(slot, u)
                with dve.Fori(0, HEADS // 2 - 1) as p:
                    for slot, u in turn(b, p):
                        unit(slot, u)
                for slot, u in turn(b, HEADS // 2 - 1, last_pair=True):
                    unit(slot, u)
                    if not slot.has_next:
                        beside_last(b, u)
                output_norm(b, 2)
                take_fold(b * HEADS + (HEADS - 1), NT - 1, 0, direct=True)
                for half in range(2):
                    output_stats(b, 3, half)
                for c in range(NK):
                    output_lo(b, 2, c)
                    if c == 1:
                        output_norm(b, 3)
                    residual(b, 0, c)
                    if not final and c > 1:
                        channel_stats(b, 1, c - 2)
                for c in range(NK):
                    output_lo(b, 3, c)
                    if not final and c == 2:
                        channel_moments(b, 1)
                    residual(b, 1, c)
                    if not final and c < 2:
                        channel_stats(b, 1, c + 2)
                if final:
                    for t in (2, 3):
                        for c in range(NK):
                            residual(b, t, c)
                else:
                    group_moments(b, 1)
                    residual(b, 2, 0)
                    group_variance(b, 1)
                    group_scale(b, 1)
                    group_norm(b, 1, 0)
                    residual(b, 2, 1)
                    group_norm(b, 1, 1)
                    group_norm(b, 1, 2)
                    residual(b, 2, 2)
                    group_norm(b, 1, 3)
                    residual(b, 2, 3)
                    residual(b, 3, 0)
                    deviations(b, 1, 0)
                    residual(b, 3, 1)
                    deviations(b, 1, 1)
                    residual(b, 3, 2)
                    layer_scale(b, 1, 0)
                    deviations(b, 1, 2)
                    residual(b, 3, 3)
                    layer_norm(b, 1, 0)
                    layer_scale(b, 1, 1)
                    deviations(b, 1, 3)
                    layer_norm(b, 1, 1)

            with dve.Fori(0, BATCH - 1) as b:
                batch(b)
            batch(BATCH - 1, final=True)

        @block.tensor
        def _(pe):
            def project(w_h, w_l, t, part, parts, full, bank=BANK_PROJ):
                w = slice(t * W, (t + 1) * W)
                terms = [(a, k, x) for k in range(NK) for a, x in ((w_h, xh), (w_l, xh), (w_h, xl))]
                n = len(terms) // parts
                for i, (a, k, x) in enumerate(terms[part * n:(part + 1) * n], part * n):
                    last = nc.tensor.matmul(ps[:, bank, :], a[:, k, :], x[:, k, w], start=(i == 0),
                                            stop=(i == len(terms) - 1))
                if part == parts - 1:
                    last.then_inc(full, 1)

            def turn_v(h, pair, t, bank=BANK_PROJ):
                pe.wait_ge(vt_ready, pair * NT + (t + 1))
                for i in range(4):
                    last = nc.tensor.transpose(ps[:, bank, i * P:(i + 1) * P],
                                               vt[:, t * W + i * P:t * W + (i + 1) * P], ident[:, :])
                last.then_inc(turn_full, 1)

            def scores_for_max(h, s, q, step, half, n):
                i, kc = divmod(step, NT)
                if step == 0 and q == 0:
                    pe.wait_ge(dup_in, h * (32 * NT) + 32 * NT)
                    pe.wait_ge(qk_lo, h * NT + NT)
                pe.wait_ge(mx_free[n % 2], half + n // 2)
                qs = q * W + i * P
                nc.tensor.matmul(ps[:, BANK_MX[n % 2], :], q_hh[s][:, qs:qs + P], k_hl[s][:, kc * W:(kc + 1) * W],
                                 start=True, stop=True).then_inc(mx_full, 1)

            def turn_max(h, q):
                pe.wait_ge(nm_ready, h * NT + (q + 1))
                nc.tensor.matmul(ps[0:4, BANK_MISC, 0:P], nm[:, q % 2, :], ident[:, :], start=True, stop=True).then_inc(nm_full, 1)

            def fold_output(slot, q):
                pe.wait_ge(ot_ready, slot.h * NT + (q + 1))
                pe.wait_ge(acc_ready, slot.units + (q + 1) * UPB)
                for i in range(4):
                    o, w = i * (DH + 1), slice(i * P, (i + 1) * P)
                    nc.tensor.matmul(ps[:, BANK_MISC, o:o + DH], ot[:, w], fold[:, :], start=True, stop=True)
                    last = nc.tensor.matmul(ps[:, BANK_MISC, o + DH:o + DH + 1], acc[:, q % 2, w], ones[:, :],
                                            start=True, stop=True)
                last.then_inc(fold_full, 1)

            def probs_times_v(slot, u):
                q, j = divmod(u, UPB)
                s = slot.odd if u >= 0 else 1 - slot.odd
                pe.wait_ge(pl_ready, slot.units + (u + 1))
                if j == 0:
                    if u == 0:
                        pe.wait_ge(v_lo, slot.h * NT + NT)
                    if u or not slot.first:
                        pe.wait_ge(ot_ready, slot.h * NT + q)
                for i in range(2):
                    v = v_hl[:, s, 2 * j + i, :]
                    nc.tensor.matmul(ps[:, BANK_PV, :], v, ph[:, u % 2, i * W:(i + 1) * W], start=(j == 0 and i == 0), stop=False)
                    last = nc.tensor.matmul(ps[:, BANK_PV, :], v, pl[:, u % 2, i * W:(i + 1) * W], start=False,
                                            stop=(j == UPB - 1 and i == 1))
                last.then_inc(pv_done, 1)

            def scores(slot, u):
                q, j = divmod(u, UPB)
                s = slot.odd
                if j == 0:
                    pe.wait_ge(row_in[q], slot.h * 16 + 16)
                w = slice(q * W, (q + 1) * W)
                for i in range(2):
                    n = 2 * u + i
                    if n > 2 or not slot.first:
                        back = 1 if n < 2 and not s else 2
                        pe.wait_ge(e_ready, slot.units * 2 + (n - back))
                    k = slice((2 * j + i) * P, (2 * j + i + 1) * P)
                    bank = BANK_S[(n + 64 * s) % 3]
                    nc.tensor.matmul(ps[:, bank, :], k_hl[s][:, k], q_hh[s][:, w], start=True, stop=False)
                    nc.tensor.matmul(ps[:, bank, :], k_h1[s][:, k], q_lm[s][:, w], start=False, stop=True).then_inc(s_ready, 1)

            def unit(slot, u):
                s = slot.odd
                scores(slot, u)
                if u >= LAG or not slot.first:
                    probs_times_v(slot, u - LAG)
                for i, (ahead, q, step) in enumerate(max_steps(slot, u)):
                    scores_for_max(slot.h + ahead, s ^ ahead, q, step, slot.mx_half, 2 * u + i)
                if u in QK_PROJ and slot.has_next:
                    t, part, parts = QK_PROJ[u]
                    if u == 0:
                        pe.wait_ge(v_lo, slot.h * NT + NT)
                        pe.wait_ge(wq_lo, slot.h + 2)
                    elif part == 0:
                        pe.wait_ge(qk_lo, slot.h * NT + (NT + t))
                    project(wq_h, wq_l, t, part, parts, qk_full)
                if u in V_PROJ[s] and slot.has_pair:
                    t, part, parts = V_PROJ[s][u]
                    if part == 0:
                        if t == 0:
                            pe.wait_ge(v_lo, slot.h * NT + 2 * NT)
                            pe.wait_ge(wv_lo, slot.pair + 2)
                        elif u == min(V_PROJ[1]):
                            pe.wait_ge(qk_lo, slot.h * NT + 2 * NT)
                        else:
                            pe.wait_ge(vt_ready, slot.pair * NT + (NT + t))
                    project(wv_h, wv_l, t, part, parts, v_full)
                if u in V_TURN[slot.odd] and slot.has_next:
                    t = V_TURN[slot.odd][u]
                    if t:
                        pe.wait_ge(v_lo, slot.h * NT + (NT + t))
                    elif not slot.odd:
                        pe.wait_ge(qk_lo, slot.h * NT + 2 * NT)
                    else:
                        pe.wait_ge(vt_ready, slot.pair * NT + 2 * NT)
                    turn_v(slot.h + 1, slot.pair + slot.odd, t)
                if u in NM_TURN:
                    ahead, q = divmod(NM_TURN[u], NT)
                    if not ahead or slot.has_next:
                        if u > AHEAD or not slot.first:
                            pe.wait_ge(o_ready, slot.h * NT + q_folded(u))
                        turn_max(slot.h + ahead, q)
                if u in FOLD and not (slot.first and u == LAG):
                    q = FOLD[u]
                    pe.wait_ge(nm_t_ready, slot.h * NT + (q + 2))
                    fold_output(slot, q)

            def q_folded(u):
                return sum(1 for v, q in FOLD.items() if v < u and q >= 0)

            def turn_outputs(b, t, k):
                n = t * NK + k
                if k == 0:
                    pe.wait_ge(on_ready, b * NT + t + 1)
                if n:
                    pe.wait_ge(aff_ready, b * (NT * NK) + n)
                for i in range(4):
                    last = nc.tensor.transpose(ps[:, BANK_TURN, i * P:(i + 1) * P], ob[:, 4 * t + i, k * P:(k + 1) * P], ident[:, :])
                last.then_inc(tr_ready, 1)

            def project_out(b, t, c):
                n = t * NK + c
                if n == 0:
                    pe.wait_ge(wo_lo, b * NK + NK)
                if n < 2:
                    pe.wait_ge(mx_free[n], b * (BATCH_MX // 2) + BATCH_MX // 2)
                else:
                    pe.wait_ge(y_ready, b * (NT * NK) + n - 1)
                if c == 0:
                    pe.wait_ge(onl_ready, b * (NT * NK) + (t + 1) * NK)
                w, cs = slice(t * W, (t + 1) * W), slice(c * P, (c + 1) * P)
                for k in range(NK):
                    nc.tensor.matmul(ps[:, BANK_OUT[n % 2], :], wo_h[:, k, cs], xh[:, k, w], start=(k == 0), stop=False)
                    nc.tensor.matmul(ps[:, BANK_OUT[n % 2], :], wo_l[:, k, cs], xh[:, k, w], start=False, stop=False)
                    last = nc.tensor.matmul(ps[:, BANK_OUT[n % 2], :], wo_h[:, k, cs], xl[:, k, w], start=False, stop=(k == NK - 1))
                last.then_inc(po_ready, 1)

            def group_sums(b, ahead, i):
                if i == 0:
                    pe.wait_ge(o_ready, (b * HEADS + ahead * HEADS) * NT)
                    pe.wait_ge(gn_in, b + (ahead + 1))
                    pe.wait_ge(bn_agg, b * (NK + 1) + (ahead * (NK + 1) + NK - 1))
                else:
                    pe.wait_ge(gn_dve, b * 4 + (ahead * 4 + 2))
                nc.tensor.matmul(ps[:, BANK_MISC, 0:NK], avg_g[:, :], (mv[:, :, 0], gs[:, :])[i], start=True, stop=True).then_inc(gn_sum, 1)

            def mean(b, ahead, t):
                if t == 0:
                    pe.wait_ge(g_ready, b * NK + (ahead * NK + NK))
                for k in range(NK):
                    last = nc.tensor.matmul(ps[:, t, :], avg_c[:, :], gb[:, k, t * W:(t + 1) * W], start=(k == 0), stop=(k == NK - 1))
                last.then_inc(mean_ready, 1)

            def variance(b, ahead, t):
                pe.wait_ge(sq_sum, b * NT + (ahead * NT + t + 1))
                if t > 1:
                    pe.wait_ge(norm_ready, b * NT + (ahead * NT + t - 1))
                for j in range(4):
                    last = nc.tensor.matmul(ps[:, BANK_VAR[t % 2], j:j + 1], sq[t % 2][:, 0, j * P:(j + 1) * P], avg_c[:, 0:1],
                                            start=True, stop=True)
                last.then_inc(var_ready, 1)

            def spread(b, ahead, t):
                pe.wait_ge(diag_ready, b * NT + (ahead * NT + t + 1))
                nc.tensor.matmul(ps[:, BANK_VAR[t % 2], :], avg_c[:, :], diag[t], start=True, stop=True).then_inc(spread_ready, 1)

            def beside_last(b, u):
                if u in OUT_TURN:
                    turn_outputs(b, *OUT_TURN[u])

            pe.wait_ge(const_ready, 2)
            pe.wait_ge(fold_ready, 1)
            for i in range(2):
                group_sums(0, 0, i)
            mean(0, 0, 0)
            mean(0, 0, 1)
            variance(0, 0, 0)
            mean(0, 0, 2)
            spread(0, 0, 0)
            variance(0, 0, 1)
            mean(0, 0, 3)
            spread(0, 0, 1)

            def batch(b, final=False):
                variance(b, 0, 2)
                spread(b, 0, 2)
                variance(b, 0, 3)
                spread(b, 0, 3)
                pe.wait_ge(wq_lo, b * HEADS + 1)
                for t, v in ((0, 0), (1, 1), (2, None), (3, 2), (None, 3)):
                    if t is not None:
                        pe.wait_ge(xl_ready, b * NT + t + 1)
                        project(wq_h, wq_l, t, 0, 1, qk_full, bank=t)
                    if v == 0:
                        pe.wait_ge(wv_lo, b * (HEADS // 2) + 1)
                    if v is not None:
                        project(wv_h, wv_l, v, 0, 1, v_full, bank=4 + v)
                pe.wait_ge(vt_ready, b * (HEADS // 2 * NT) + 2)
                for n in range(PRO_MX):
                    if n in PRO_TURN:
                        turn_v(b * HEADS, b * (HEADS // 2), PRO_TURN[n], bank=PRO_TURN[n])
                    q, step = divmod(n, 16)
                    scores_for_max(b * HEADS, 0, q, step, b * (BATCH_MX // 2), n)
                    if n == 15:
                        turn_max(b * HEADS, 0)
                pe.wait_ge(rows_set, (b + 1) * 4)
                pe.wait_ge(v_lo, b * (HEADS * NT) + NT)
                for slot, u in opening(b):
                    unit(slot, u)
                with pe.Fori(0, HEADS // 2 - 1) as p:
                    for slot, u in turn(b, p):
                        unit(slot, u)
                for slot, u in turn(b, HEADS // 2 - 1, last_pair=True):
                    unit(slot, u)
                    if not slot.has_next:
                        beside_last(b, u)
                after = Slot(b + 1, 0, 0)
                for u in range(-LAG, 0):
                    probs_times_v(after, u)
                beside_out = {divmod(1 + n, NK): divmod(OUT_EARLY * NK + n, NK) for n in range((NT - OUT_EARLY) * NK)}
                for t in range(NT - 1):
                    for c in range(NK):
                        if (t, c) in beside_out:
                            turn_outputs(b, *beside_out[t, c])
                        if not final and t == 2 and c < 2:
                            group_sums(b, 1, c)
                        project_out(b, t, c)
                        if (t, c) == (0, 0):
                            fold_output(after, -1)
                if final:
                    for c in range(NK):
                        project_out(b, 3, c)
                else:
                    project_out(b, 3, 0)
                    mean(b, 1, 0)
                    project_out(b, 3, 1)
                    mean(b, 1, 1)
                    project_out(b, 3, 2)
                    variance(b, 1, 0)
                    mean(b, 1, 2)
                    project_out(b, 3, 3)
                    spread(b, 1, 0)
                    variance(b, 1, 1)
                    mean(b, 1, 3)
                    spread(b, 1, 1)

            with pe.Fori(0, BATCH - 1) as b:
                batch(b)
            batch(BATCH - 1, final=True)


_INS = ["x", "L0_conv_w_qkv", "L0_conv_b_qkv", "L0_conv_w_out", "L0_conv_b_out", "L0_conv_gamma1", "L0_conv_beta1",
        "L0_conv_gamma2", "L0_conv_beta2"]


def kernel(**inputs):
    import numpy as _np
    import concourse.bacc as _bacc
    from concourse import mybir as _mybir
    from concourse.bass_utils import run_bass_kernel_spmd as _run

    nc = _bacc.Bacc("TRN2", target_bir_lowering=False, num_devices=1)
    arrays, args = {}, []
    for name in _INS:
        a = _np.ascontiguousarray(inputs[name])
        arrays[f"in_{name}_dram"] = a
        args.append(nc.dram_tensor(f"in_{name}_dram", a.shape, _mybir.dt.from_np(a.dtype), kind="ExternalInput").ap())
    args.append(nc.dram_tensor("out_0_dram", (4, 512, 64, 32), _mybir.dt.float32, kind="ExternalOutput").ap())
    program(nc, *args)
    r = _run(nc, [arrays], core_ids=[0])
    return r.results[0]["out_0_dram"]
```
